# Optimizing a Trainium2 kernel written in Bass

```python
import numpy as np
import jax
import jax.numpy as jnp

def _softmax(x, axis=-1):
    return jax.nn.softmax(x, axis=axis)

def _gelu(x):
    return jax.nn.gelu(x, approximate=True)

def _silu(x):
    return jax.nn.silu(x)

def _sigmoid(x):
    return jax.nn.sigmoid(x)

def _layernorm(x, axis=-1, eps=1e-05):
    m = jnp.mean(x, axis=axis, keepdims=True)
    v = jnp.var(x, axis=axis, keepdims=True)
    return (x - m) / jnp.sqrt(v + eps)

def _scatter_add(tgt, idx, src, axis=0):
    return tgt.at[idx].add(src)

def _segment_sum(src, seg, n):
    return jax.ops.segment_sum(src, seg, n)
kernel_name = 'mk_decoder_preln_d2_seqx_r8_9c981f'

def setup_inputs(seed: int=0):
    np.random.seed(seed)
    _w = jnp.asarray

    def _rec_inputs():
        import jax
        import jax.numpy as jnp
        _rk = jax.random.key(seed)
        x = -0.0002928 + 1 * jax.random.normal(jax.random.fold_in(_rk, 1), (2, 512, 128), jnp.float32)
        _lenS = 512 - jax.random.randint(jax.random.fold_in(_rk, 7), (2,), 0, max(1, 512 // 4) + 1, jnp.int32)
        _lenS2 = 77 - jax.random.randint(jax.random.fold_in(_rk, 8), (2,), 0, max(1, 77 // 4) + 1, jnp.int32)
        _ctx_1024P = jax.random.normal(jax.random.fold_in(_rk, 11), (2, 16, 128), jnp.float32)
        _ctx_1024c = jax.random.dirichlet(jax.random.fold_in(_rk, 511), 0.3 * jnp.ones((16,), jnp.float32), (2, 77))
        _ctx_1024t = jnp.einsum('bsk,bkd->bsd', _ctx_1024c, _ctx_1024P)
        _ctx_1024t = _ctx_1024t * jax.lax.rsqrt(jnp.mean(jnp.square(_ctx_1024t)) + 1e-12) * 0.953939
        ctx_1024 = 4.13588e-05 + 0.999923 * (_ctx_1024t + 0.3 * jax.random.normal(jax.random.fold_in(_rk, 611), (2, 77, 128), jnp.float32))
        _validS = jnp.arange(512)[None, :] < _lenS[:, None]
        _validS2 = jnp.arange(77)[None, :] < _lenS2[:, None]
        _causal = jnp.tril(jnp.ones((512, 512), dtype=bool))
        mask_BxS2_bk0 = jnp.logical_not(jnp.broadcast_to(_validS2[:, :], (2, 77)))
        return (x, ctx_1024, _lenS2, mask_BxS2_bk0)
    x, ctx_1024, _lenS2, mask_BxS2_bk0 = _rec_inputs()

    def _L0_attn_setup():
        import jax, jax.numpy as jnp
        import numpy as np
        N_HEAD = 16
        HEAD_SIZE = 128
        EMBED = 128
        MULTI_HEAD_SIZE = HEAD_SIZE // N_HEAD
        B, S = (4, 256)
        key = jax.random.key(seed)
        k1, k2, k3, k4 = jax.random.split(key, 4)
        x = jax.random.normal(k1, (B, S, EMBED), dtype=jnp.float32)
        w_qkv = jax.random.normal(k2, (3 * HEAD_SIZE, EMBED), dtype=jnp.float32) * 0.02
        w_proj = jax.random.normal(k3, (EMBED, HEAD_SIZE), dtype=jnp.float32) * 0.02
        b_proj = jax.random.normal(k4, (EMBED,), dtype=jnp.float32) * 0.02
        return {'x': x, 'w_qkv': w_qkv, 'w_proj': w_proj, 'b_proj': b_proj}
    _L0_attn_all = _L0_attn_setup()
    _L0_attn_in = {k: v for k, v in _L0_attn_all.items() if k in ('w_qkv', 'w_proj', 'b_proj')}
    del _L0_attn_all

    def _L0_xattn_setup():
        import jax, jax.numpy as jnp
        import numpy as np
        DIM = 128
        HEADS = 16
        HEAD_DIM = DIM // HEADS
        SCALE = HEAD_DIM ** (-0.5)
        B, N_TGT, N_SRC = (4, 128, 256)
        key = jax.random.key(seed)
        ks = jax.random.split(key, 8)
        s = 0.02
        tgt = jax.random.normal(ks[0], (B, N_TGT, DIM), dtype=jnp.float32)
        src = jax.random.normal(ks[1], (B, N_SRC, DIM), dtype=jnp.float32)
        src_padded_mask = jnp.broadcast_to(jnp.arange(N_SRC) >= N_SRC - 64, (B, N_SRC))
        q_w = jax.random.normal(ks[2], (DIM, DIM), dtype=jnp.float32) * s
        q_b = jnp.zeros((DIM,), dtype=jnp.float32)
        kv_w = jax.random.normal(ks[3], (2 * DIM, DIM), dtype=jnp.float32) * s
        kv_b = jnp.zeros((2 * DIM,), dtype=jnp.float32)
        proj_w = jax.random.normal(ks[4], (DIM, DIM), dtype=jnp.float32) * s
        proj_b = jnp.zeros((DIM,), dtype=jnp.float32)
        return {'tgt': tgt, 'src': src, 'src_padded_mask': src_padded_mask, 'q_w': q_w, 'q_b': q_b, 'kv_w': kv_w, 'kv_b': kv_b, 'proj_w': proj_w, 'proj_b': proj_b}
    _L0_xattn_all = _L0_xattn_setup()
    _L0_xattn_in = {k: v for k, v in _L0_xattn_all.items() if k in ('q_w', 'q_b', 'kv_w', 'kv_b', 'proj_w', 'proj_b')}
    del _L0_xattn_all

    def _L0_ffn_setup():
        import jax, jax.numpy as jnp
        import numpy as np
        E = 8
        D = 128
        H = 256
        TOP_K = 2
        key = jax.random.key(seed)
        k_x, k_g, k_w1, k_w2 = jax.random.split(key, 4)
        B, S = (4, 256)
        inp = {'input': jax.random.normal(k_x, (B, S, D), dtype=jnp.float32), 'Wg': jax.random.normal(k_g, (D, E), dtype=jnp.float32) * 0.02, 'W1': jax.random.normal(k_w1, (E, D, H), dtype=jnp.float32) * 0.02, 'b1': jnp.zeros((E, H), dtype=jnp.float32), 'W2': jax.random.normal(k_w2, (E, H, D), dtype=jnp.float32) * 0.02, 'b2': jnp.zeros((E, D), dtype=jnp.float32)}
        return inp
    _L0_ffn_all = _L0_ffn_setup()
    _L0_ffn_in = {k: v for k, v in _L0_ffn_all.items() if k in ('Wg', 'W1', 'b1', 'W2', 'b2')}
    del _L0_ffn_all

    def _L1_attn_setup():
        import jax, jax.numpy as jnp
        import numpy as np
        B, S, E, H = (2, 256, 128, 16)
        D = E // H
        EPS = 1e-06

        def _angle_decay():
            a = 1.0 / 10000.0 ** jnp.linspace(0.0, 1.0, D // 2)
            angle = jnp.repeat(a, 2)
            decay = jnp.log(1.0 - 2.0 ** (-5.0 - jnp.arange(H, dtype=jnp.float32)))
            return (angle, decay)

        def _rel_pos(slen):
            angle, decay = _angle_decay()
            idx = jnp.arange(slen, dtype=jnp.float32)
            sin = jnp.sin(idx[:, None] * angle[None, :])
            cos = jnp.cos(idx[:, None] * angle[None, :])
            diff = idx[:, None] - idx[None, :]
            tril = diff >= 0
            masked = jnp.where(tril, diff, jnp.inf)
            mask = jnp.exp(masked * decay[:, None, None])
            mask = jnp.nan_to_num(mask)
            mask = mask / jnp.sqrt(jnp.sum(mask, axis=-1, keepdims=True))
            return (sin, cos, mask)

        def _rotate_every_two(x):
            x1 = x[..., ::2]
            x2 = x[..., 1::2]
            return jnp.stack((-x2, x1), axis=-1).reshape(x.shape)

        def _theta_shift(x, sin, cos):
            return x * cos + _rotate_every_two(x) * sin
        key = jax.random.key(seed)
        ks = jax.random.split(key, 5)
        scale = 1.0 / np.sqrt(E)
        return {'x': jax.random.normal(ks[0], (B, S, E), dtype=jnp.float32), 'Wq': jax.random.normal(ks[1], (E, E), dtype=jnp.float32) * scale, 'Wk': jax.random.normal(ks[2], (E, E), dtype=jnp.float32) * scale, 'Wv': jax.random.normal(ks[3], (E, E), dtype=jnp.float32) * scale, 'Wg': jax.random.normal(ks[4], (E, E), dtype=jnp.float32) * scale}
    _L1_attn_all = _L1_attn_setup()
    _L1_attn_in = {k: v for k, v in _L1_attn_all.items() if k in ('Wq', 'Wk', 'Wv', 'Wg')}
    del _L1_attn_all

    def _L1_xattn_setup():
        import jax, jax.numpy as jnp
        import numpy as np
        N_HEADS = 16
        key = jax.random.key(seed)
        ks = jax.random.split(key, 9)
        B, T, C, S = (32, 8, 128, 512)
        w_scale = 1.0 / np.sqrt(C).astype(np.float32)
        return {'x': jax.random.normal(ks[0], (B, T, C), jnp.float32), 'cache_k': jax.random.normal(ks[1], (B, S, C), jnp.float32), 'cache_v': jax.random.normal(ks[2], (B, S, C), jnp.float32), 'cache_len': jax.random.randint(ks[3], (B,), 0, S - T, jnp.int32), 'wq': jax.random.normal(ks[4], (C, C), jnp.float32) * w_scale, 'wk': jax.random.normal(ks[5], (C, C), jnp.float32) * w_scale, 'wv': jax.random.normal(ks[6], (C, C), jnp.float32) * w_scale, 'wo': jax.random.normal(ks[7], (C, C), jnp.float32) * w_scale, 'bo': jnp.zeros((C,), jnp.float32)}
    _L1_xattn_all = _L1_xattn_setup()
    _L1_xattn_in = {k: v for k, v in _L1_xattn_all.items() if k in ('wq', 'wk', 'wv', 'wo', 'bo')}
    del _L1_xattn_all

    def _L1_ffn_setup():
        import jax, jax.numpy as jnp
        import numpy as np
        B, S, D_MODEL, D_FF = (4, 256, 128, 512)

        def _quantum_transform(hidden, theta, w_real, w_imag):
            imag = w_imag * jnp.sin(theta + hidden * 0.1)
            quantum_phase = jnp.cos(theta) * w_real + jnp.sin(theta) * w_imag
            return hidden + quantum_phase * imag * 0.1
        key = jax.random.key(seed)
        ks = jax.random.split(key, 8)
        return {'x': jax.random.normal(ks[0], (B, S, D_MODEL), dtype=jnp.float32), 'W1': jax.random.normal(ks[1], (D_MODEL, D_FF), dtype=jnp.float32) * (1.0 / np.sqrt(D_MODEL)), 'b1': jnp.zeros((D_FF,), dtype=jnp.float32), 'quantum_phases': jax.random.normal(ks[2], (D_FF,), dtype=jnp.float32) * (2.0 * np.pi), 'quantum_weights_real': jax.random.normal(ks[3], (D_FF,), dtype=jnp.float32) * 0.1, 'quantum_weights_imag': jax.random.normal(ks[4], (D_FF,), dtype=jnp.float32) * 0.1, 'W2': jax.random.normal(ks[5], (D_FF, D_MODEL), dtype=jnp.float32) * (1.0 / np.sqrt(D_FF)), 'b2': jnp.zeros((D_MODEL,), dtype=jnp.float32)}
    _L1_ffn_all = _L1_ffn_setup()
    _L1_ffn_in = {k: v for k, v in _L1_ffn_all.items() if k in ('W1', 'b1', 'quantum_phases', 'quantum_weights_real', 'quantum_weights_imag', 'W2', 'b2')}
    del _L1_ffn_all
    return {'x': x, 'ctx_1024': ctx_1024, '_lenS2': _lenS2, 'mask_BxS2_bk0': mask_BxS2_bk0, 'L0_attn_w_qkv': _L0_attn_in['w_qkv'], 'L0_attn_w_proj': _L0_attn_in['w_proj'], 'L0_attn_b_proj': _L0_attn_in['b_proj'], 'L0_xattn_q_w': _L0_xattn_in['q_w'], 'L0_xattn_q_b': _L0_xattn_in['q_b'], 'L0_xattn_kv_w': _L0_xattn_in['kv_w'], 'L0_xattn_kv_b': _L0_xattn_in['kv_b'], 'L0_xattn_proj_w': _L0_xattn_in['proj_w'], 'L0_xattn_proj_b': _L0_xattn_in['proj_b'], 'L0_ffn_Wg': _L0_ffn_in['Wg'], 'L0_ffn_W1': _L0_ffn_in['W1'], 'L0_ffn_b1': _L0_ffn_in['b1'], 'L0_ffn_W2': _L0_ffn_in['W2'], 'L0_ffn_b2': _L0_ffn_in['b2'], 'L1_attn_Wq': _L1_attn_in['Wq'], 'L1_attn_Wk': _L1_attn_in['Wk'], 'L1_attn_Wv': _L1_attn_in['Wv'], 'L1_attn_Wg': _L1_attn_in['Wg'], 'L1_xattn_wq': _L1_xattn_in['wq'], 'L1_xattn_wk': _L1_xattn_in['wk'], 'L1_xattn_wv': _L1_xattn_in['wv'], 'L1_xattn_wo': _L1_xattn_in['wo'], 'L1_xattn_bo': _L1_xattn_in['bo'], 'L1_ffn_W1': _L1_ffn_in['W1'], 'L1_ffn_b1': _L1_ffn_in['b1'], 'L1_ffn_quantum_phases': _L1_ffn_in['quantum_phases'], 'L1_ffn_quantum_weights_real': _L1_ffn_in['quantum_weights_real'], 'L1_ffn_quantum_weights_imag': _L1_ffn_in['quantum_weights_imag'], 'L1_ffn_W2': _L1_ffn_in['W2'], 'L1_ffn_b2': _L1_ffn_in['b2']}

def reference(x, ctx_1024, _lenS2, mask_BxS2_bk0, L0_attn_w_qkv, L0_attn_w_proj, L0_attn_b_proj, L0_xattn_q_w, L0_xattn_q_b, L0_xattn_kv_w, L0_xattn_kv_b, L0_xattn_proj_w, L0_xattn_proj_b, L0_ffn_Wg, L0_ffn_W1, L0_ffn_b1, L0_ffn_W2, L0_ffn_b2, L1_attn_Wq, L1_attn_Wk, L1_attn_Wv, L1_attn_Wg, L1_xattn_wq, L1_xattn_wk, L1_xattn_wv, L1_xattn_wo, L1_xattn_bo, L1_ffn_W1, L1_ffn_b1, L1_ffn_quantum_phases, L1_ffn_quantum_weights_real, L1_ffn_quantum_weights_imag, L1_ffn_W2, L1_ffn_b2):
    import jax
    import jax.numpy as jnp

    def _L0_attn_ref(x, w_qkv, w_proj, b_proj):
        import jax, jax.numpy as jnp
        import numpy as np
        N_HEAD = 16
        HEAD_SIZE = 128
        EMBED = 128
        MULTI_HEAD_SIZE = HEAD_SIZE // N_HEAD
        B, S = (4, 256)
        qkv = jnp.einsum('bse,he->bsh', x, w_qkv)
        q, k, v = jnp.split(qkv, 3, axis=-1)
        scale = 1.0 / np.sqrt(MULTI_HEAD_SIZE).astype(np.float32)
        scores = jnp.einsum('bqh,bkh->bqk', q, k) * scale
        probs = jax.nn.softmax(scores, axis=-1)
        out = jnp.einsum('bqk,bkh->bqh', probs, v)
        Bn, Sn, H = out.shape
        out = jnp.swapaxes(out, 1, 2).reshape(Bn, Sn, H)
        out = jnp.einsum('bsh,eh->bse', out, w_proj) + b_proj
        return out

    def _L0_xattn_ref(tgt, src, src_padded_mask, q_w, q_b, kv_w, kv_b, proj_w, proj_b):
        import jax, jax.numpy as jnp
        import numpy as np
        DIM = 128
        HEADS = 16
        HEAD_DIM = DIM // HEADS
        SCALE = HEAD_DIM ** (-0.5)
        B, N_TGT, N_SRC = (4, 128, 256)
        Bb, Ns, C = src.shape
        Nt = tgt.shape[1]
        kv = (src @ kv_w.T + kv_b).reshape(Bb, Ns, 2, HEADS, HEAD_DIM)
        kv = jnp.transpose(kv, (2, 0, 3, 1, 4))
        k, v = (kv[0], kv[1])
        q = (tgt @ q_w.T + q_b).reshape(Bb, Nt, HEADS, HEAD_DIM).transpose(0, 2, 1, 3)
        attn = jnp.einsum('bhqd,bhkd->bhqk', q, k) * SCALE
        attn = jnp.where(src_padded_mask[:, None, None, :], -jnp.inf, attn)
        attn = jax.nn.softmax(attn, axis=-1)
        out = jnp.einsum('bhqk,bhkd->bhqd', attn, v)
        out = out.transpose(0, 2, 1, 3).reshape(Bb, Nt, C)
        out = out @ proj_w.T + proj_b
        return out

    def _L0_ffn_ref(input, Wg, W1, b1, W2, b2):
        import jax, jax.numpy as jnp
        import numpy as np
        E = 8
        D = 128
        H = 256
        TOP_K = 2
        logits = jnp.einsum('bsd,de->bse', input, Wg)
        probs = jax.nn.softmax(logits, axis=-1)
        top_vals, top_idx = jax.lax.top_k(probs, TOP_K)
        top_vals = top_vals / jnp.sum(top_vals, axis=-1, keepdims=True)
        onehot = jax.nn.one_hot(top_idx, E, dtype=input.dtype)
        mask = jnp.sum(onehot, axis=2)
        scores = jnp.sum(onehot * top_vals[..., None], axis=2)
        xm = input[None] * jnp.moveaxis(mask, -1, 0)[..., None]
        h = jnp.einsum('ebsd,edh->ebsh', xm, W1) + b1[:, None, None, :]
        h = jax.nn.relu(h)
        y = jnp.einsum('ebsh,ehd->ebsd', h, W2) + b2[:, None, None, :]
        out = jnp.sum(y * jnp.moveaxis(scores, -1, 0)[..., None], axis=0)
        return out

    def _L1_attn_ref(x, Wq, Wk, Wv, Wg):
        import jax, jax.numpy as jnp
        import numpy as np
        B, S, E, H = (2, 256, 128, 16)
        D = E // H
        EPS = 1e-06

        def _angle_decay():
            a = 1.0 / 10000.0 ** jnp.linspace(0.0, 1.0, D // 2)
            angle = jnp.repeat(a, 2)
            decay = jnp.log(1.0 - 2.0 ** (-5.0 - jnp.arange(H, dtype=jnp.float32)))
            return (angle, decay)

        def _rel_pos(slen):
            angle, decay = _angle_decay()
            idx = jnp.arange(slen, dtype=jnp.float32)
            sin = jnp.sin(idx[:, None] * angle[None, :])
            cos = jnp.cos(idx[:, None] * angle[None, :])
            diff = idx[:, None] - idx[None, :]
            tril = diff >= 0
            masked = jnp.where(tril, diff, jnp.inf)
            mask = jnp.exp(masked * decay[:, None, None])
            mask = jnp.nan_to_num(mask)
            mask = mask / jnp.sqrt(jnp.sum(mask, axis=-1, keepdims=True))
            return (sin, cos, mask)

        def _rotate_every_two(x):
            x1 = x[..., ::2]
            x2 = x[..., 1::2]
            return jnp.stack((-x2, x1), axis=-1).reshape(x.shape)

        def _theta_shift(x, sin, cos):
            return x * cos + _rotate_every_two(x) * sin
        bsz, tgt_len, _ = x.shape
        sin, cos, mask = _rel_pos(tgt_len)
        scaling = E ** (-0.5)
        q = x @ Wq
        k = x @ Wk * scaling
        v = x @ Wv
        g = x @ Wg
        q = q.reshape(bsz, tgt_len, H, D).transpose(0, 2, 1, 3)
        k = k.reshape(bsz, tgt_len, H, D).transpose(0, 2, 1, 3)
        vr = v.reshape(bsz, tgt_len, H, D).transpose(0, 2, 1, 3)
        qr = _theta_shift(q, sin, cos)
        kr = _theta_shift(k, sin, cos)
        qk = jnp.einsum('bhqd,bhkd->bhqk', qr, kr) * mask[None]
        denom = jax.lax.stop_gradient(jnp.clip(jnp.sum(jnp.abs(qk), axis=-1, keepdims=True), 1.0, 50000.0))
        out = jnp.einsum('bhqk,bhkd->bhqd', qk / denom, vr)
        out = out.transpose(0, 2, 1, 3)
        out = out * jax.lax.rsqrt(jnp.mean(out * out, axis=-1, keepdims=True) + EPS)
        out = out.reshape(bsz, tgt_len, E)
        return jax.nn.silu(g) * out

    def _L1_xattn_ref(x, cache_k, cache_v, cache_len, wq, wk, wv, wo, bo):
        import jax, jax.numpy as jnp
        import numpy as np
        N_HEADS = 16
        B, T, C = x.shape
        S = cache_k.shape[1]
        H = N_HEADS
        hd = C // H
        q = x @ wq.T
        k_new = x @ wk.T
        v_new = x @ wv.T
        pos = jnp.arange(S)
        past_mask = (pos[None, :] < cache_len[:, None])[..., None]
        past_k = jnp.where(past_mask, cache_k, 0.0)
        past_v = jnp.where(past_mask, cache_v, 0.0)
        k = jnp.concatenate([past_k, k_new], axis=1)
        v = jnp.concatenate([past_v, v_new], axis=1)

        def to_heads(t):
            return t.reshape(B, t.shape[1], H, hd).transpose(0, 2, 1, 3)
        qh, kh, vh = (to_heads(q), to_heads(k), to_heads(v))
        scores = jnp.einsum('bhqd,bhkd->bhqk', qh, kh) / np.sqrt(hd).astype(np.float32)
        max_cl = jnp.max(cache_len)
        key_valid = jnp.concatenate([pos < max_cl, jnp.ones((T,), bool)])
        NEG = jnp.float32(-1e+30)
        scores = jnp.where(key_valid[None, None, None, :], scores, NEG)
        attn = jax.nn.softmax(scores, axis=-1)
        out = jnp.einsum('bhqk,bhkd->bhqd', attn, vh)
        out = out.transpose(0, 2, 1, 3).reshape(B, T, C)
        return out @ wo.T + bo

    def _L1_ffn_ref(x, W1, b1, quantum_phases, quantum_weights_real, quantum_weights_imag, W2, b2):
        import jax, jax.numpy as jnp
        import numpy as np
        B, S, D_MODEL, D_FF = (4, 256, 128, 512)

        def _quantum_transform(hidden, theta, w_real, w_imag):
            imag = w_imag * jnp.sin(theta + hidden * 0.1)
            quantum_phase = jnp.cos(theta) * w_real + jnp.sin(theta) * w_imag
            return hidden + quantum_phase * imag * 0.1
        hidden = jnp.einsum('bsd,df->bsf', x, W1) + b1
        q = _quantum_transform(hidden, quantum_phases, quantum_weights_real, quantum_weights_imag)
        act = jax.nn.relu(q)
        return jnp.einsum('bsf,fd->bsd', act, W2) + b2
    x = x + _L0_attn_ref(_layernorm(x, axis=-1), L0_attn_w_qkv, L0_attn_w_proj, L0_attn_b_proj)
    x = x + _L0_xattn_ref(_layernorm(x, axis=-1), ctx_1024, mask_BxS2_bk0, L0_xattn_q_w, L0_xattn_q_b, L0_xattn_kv_w, L0_xattn_kv_b, L0_xattn_proj_w, L0_xattn_proj_b)
    x = x + _L0_ffn_ref(_layernorm(x, axis=-1), L0_ffn_Wg, L0_ffn_W1, L0_ffn_b1, L0_ffn_W2, L0_ffn_b2)
    x = x + _L1_attn_ref(_layernorm(x, axis=-1), L1_attn_Wq, L1_attn_Wk, L1_attn_Wv, L1_attn_Wg)
    x = x + _L1_xattn_ref(_layernorm(x, axis=-1), ctx_1024, ctx_1024, _lenS2, L1_xattn_wq, L1_xattn_wk, L1_xattn_wv, L1_xattn_wo, L1_xattn_bo)
    x = x + _L1_ffn_ref(_layernorm(x, axis=-1), L1_ffn_W1, L1_ffn_b1, L1_ffn_quantum_phases, L1_ffn_quantum_weights_real, L1_ffn_quantum_weights_imag, L1_ffn_W2, L1_ffn_b2)
    return x

_drawn_inputs = setup_inputs


def setup_inputs(seed=0):
    import zlib

    import numpy as np

    out = dict(_drawn_inputs(seed))
    spreads = {'L0_xattn_q_b': (0.0, 2.0),
     'L0_xattn_kv_b': (0.0, 0.8),
     'L0_xattn_proj_b': (0.0, 0.1),
     'L0_ffn_b1': (0.0, 1.66),
     'L0_ffn_b2': (0.0, 0.354),
     'L1_xattn_bo': (0.0, 0.269),
     'L1_ffn_b1': (0.0, 0.397),
     'L1_ffn_b2': (0.0, 0.329)}
    factors = {'L0_attn_w_qkv': 8.0,
     'L0_attn_w_proj': 8.0,
     'L0_xattn_q_w': 64.0,
     'L1_ffn_quantum_phases': 45.756,
     'L1_ffn_quantum_weights_real': 64.0,
     'L1_ffn_quantum_weights_imag': 36.835,
     'L0_attn_b_proj': 7.669,
     'L0_xattn_kv_w': 6.202,
     'L0_xattn_proj_w': 5.263,
     'L0_ffn_W1': 5.064}
    for name, (base, spread) in spreads.items():
        noise = np.random.default_rng([zlib.crc32(name.encode()), seed]).standard_normal(out[name].shape)
        drawn = base * np.exp(spread * noise) if base else spread * noise
        out[name] = jnp.asarray(drawn.astype(out[name].dtype))
    for name, factor in factors.items():
        out[name] = (out[name] * factor).astype(out[name].dtype)
    return out
```

```python
from contextlib import ExitStack

import numpy as np

import concourse.bass as bass
from concourse import mybir

F32 = mybir.dt.float32
F16 = mybir.dt.float16
U8 = mybir.dt.uint8
I32 = mybir.dt.int32
ALU = mybir.AluOpType
ACT = mybir.ActivationFunctionType
AX = mybir.AxisListType

B, S, D = 2, 512, 128
NC = S // 128
H, HD, G, SL = 16, 8, 4, 4
KC = 77
NE, FE = 8, 256
FF = 512
NJ = FF // 128
SCALE = HD ** -0.5
BIG = 60000.0
LN_EPS = 1e-5
RMS_EPS = 1e-6
ROUND = 1.5 * 2.0 ** 23
TWO_PI = 2.0 * np.pi
PI_A = 6.28125
PI_B = float(np.float32(np.round((TWO_PI - PI_A) * 2 ** 21) / 2 ** 21))
PI_C = float(np.float32(TWO_PI - PI_A - PI_B))
TURN = float(np.nextafter(np.float32(TWO_PI), np.float32(0)))
PK = S + KC
VW = H * (HD + 1) + 32 - (HD + 1)
KR = 4
LAST = 6

CHUNKS = [
    [("ident", 128), ("a_wq", 128), ("a_wk", 128), ("a_wv", 128), ("a_wp", 128), ("a_bp", 128)],
    [("b_wq", 128), ("b_wk", 128), ("b_wv", 128), ("b_wp", 128), ("b_bp", 128), ("b_vb", 128),
     ("b_qb", 1), ("b_kb", 1), ("kconst", 1), ("kmask", 1), ("qconst", 1), ("pos", 1),
     ("posrow", KC), ("ctxT", B * KC)],
    [("c_wg", NE), ("c_b1", 2 * NE), ("c_reset", NC * NE), ("c_b2", 128), ("c_w1", NE * FE)],
    [("c_w2", NE * FE)],
    [("d_wq", 128), ("d_wqs", 128), ("d_wk", 128), ("d_wks", 128), ("d_wv", 128), ("d_wg", 128),
     ("d_cosq", S), ("d_sinq", S), ("d_cosk", S), ("d_sink", S)],
    [("d_tri", 128), ("d_gm", 128), ("d_tn", NC * H), ("d_td", NC * H), ("d_one", NC * VW)],
    [("e_wq", 128), ("e_wk", 128), ("e_wv", 128), ("e_wo", 128), ("e_bo", 128),
     ("f_b2", 128), ("f_b1", NJ), ("f_th", NJ), ("f_wr", NJ), ("f_wi", NJ),
     ("f_w1", FF), ("f_w2", FF)],
]
WIDTH = sum(n for ch in CHUNKS for _, n in ch)
LATE = sum(n for _, n in CHUNKS[-1])
assert LATE <= NE * FE
HALVES = [("ident16", 128), ("q_hi", SL * 128), ("q_lo", SL * 128), ("k_hi", SL * 128), ("k_lo", SL * 128),
          ("sel_e", NE * 128)]
HWIDTH = sum(n for _, n in HALVES)


def offsets(pairs):
    at, out = 0, {}
    for name, n in pairs:
        out[name] = (at, at + n)
        at += n
    return out


def decoder(nc, x, ctx_kd, lens, maskb, par, half, out):
    P32 = offsets([p for ch in CHUNKS for p in ch])
    P16 = offsets(HALVES)
    stack = ExitStack()
    with stack:
        def sb(name, shape, dt=F32):
            return stack.enter_context(nc.sbuf_tensor(name, shape, dt))

        def sem(name):
            return stack.enter_context(nc.semaphore(name))

        params = sb("params", [128, WIDTH - LATE])
        halves = sb("halves", [128, HWIDTH], F16)

        for name, _ in CHUNKS[-1]:
            P32[name] = tuple(a - (WIDTH - LATE) + P32["c_w1"][0] for a in P32[name])

        def par_of(name):
            return params[:, P32[name][0]:P32[name][1]]

        def half_of(name):
            return halves[:, P16[name][0]:P16[name][1]]

        ident = par_of("ident")
        ident16 = half_of("ident16")

        X = sb("X", [128, B, NC, 128])
        R = sb("R", [128, B, NC, 128])
        ctxk = sb("ctxk", [KC, B, 128])
        lens_i = sb("lens_i", [128, B], I32)
        mask_u = sb("mask_u", [128, B, KC], U8)
        bn = sb("bn", [128, B, NC, 6])
        mv = sb("mv", [128, B, NC, 2])
        veps = sb("veps", [128, B, NC])
        rstd = sb("rstd", [128, B, NC])
        neghalf = sb("neghalf", [128, B * NC * H])
        xn = sb("xn", [128, B, NC, 128])
        xnT = sb("xnT", [128, B, S])
        qT = sb("qT", [128, B, S])
        kT = sb("kT", [128, B, S])
        vtok = sb("vtok", [128, B, NC, 128])
        negmax = sb("negmax", [128, B, NC])
        rowsum = sb("rowsum", [128, B, NC])
        rinv = sb("rinv", [128, B, NC])
        big = sb("big", [128, 16, 512])
        PT = sb("PT", [128, 8, 512])
        Osb = sb("Osb", [128, B, NC, 128])
        hi_flat = sb("hi", [128, B * 2 * PK], F16)
        hi = hi_flat[:, :].rearrange("p (b w k) -> p b w k", b=B, w=2)
        lo = sb("lo", [128, B, 2, PK], F16)
        qst = sb("qst", [128, B, SL, S], F16)
        kst = sb("kst", [128, B, SL, S], F16)
        kbd = sb("kbd", [128, B, SL, G * KC], F16)
        kadd = sb("kadd", [128, B, KC], F32)
        kw = sb("kw", [128, KR, G, S], F16)
        vst = sb("vst", [128, B, NC + 1, VW])
        vhead = vst[:, :, :, 0:H * (HD + 1)].rearrange("p b c (h j) -> p b c h j", h=H)
        Mx = sb("Mx", [128, B, SL, NC, 128], F16)
        Mp = sb("Mp", [128, B, NC * G])
        Mn = sb("Mn", [128, B, NC * G])
        oT = PT[:, :, :].rearrange("p (b s) q -> p b s q", b=B)
        rden = sb("rden", [128, B, NC, SL, G])
        on, onT = Osb, qT
        lens_f = sb("lens_f", [128, B])
        maxlen = sb("maxlen", [128, 1])
        kpast = sb("kpast", [128, B, KC])
        posm = sb("posm", [128, B, KC])
        vkeep = sb("vkeep", [128, B])
        small = [sb(f"small{n}", [128, B, NC, NE]) for n in range(10)]
        thin = [sb(f"thin{n}", [128, B, NC]) for n in range(3)]
        s16 = kst[:, :, 0]
        s32 = kT[0:NE]
        rot = PT[:, 0:4, :].rearrange("p (b w) q -> p b w q", b=B)
        ktok = Osb
        spare = par_of("c_w2")
        th = spare[:, 0:1024].rearrange("p (b c d) -> p b c d", b=B, c=NC)
        state = spare[:, 1024:1792].rearrange("p (b c d) -> p b c d", b=B, c=3)
        stmp = spare[:, 1792:2048].rearrange("p (b d) -> p b d", b=B)
        cross = onT[:, :, :].rearrange("p b (c d) -> p b c d", c=NC)
        f16h = [sb(f"fh{n}", [128, B, NC * H]) for n in range(6)]
        Aoff = [sb(f"Aoff{n}", [128, 768])[:, :] for n in range(2)]
        Aoff.append(hi_flat[:, 0:1536].bitcast(F32))
        Aoff.append(R[:, :, :, :].rearrange("p b c d -> p (b c d)")[:, 0:768])
        tv = [sb(f"tv{n}", [128, NJ]) for n in range(12)]

        pair = [stack.enter_context(nc.psum_tensor(f"pair{n}", [128, 2, 512], F32)) for n in range(2)]
        one = [stack.enter_context(nc.psum_tensor(f"one{n}", [128, 512], F32)) for n in range(4)]
        filled = [sem(f"filled{n}") for n in range(6)]
        drained = [sem(f"drained{n}") for n in range(6)]

        class Tile:
            pass

        tiles, uses, turn = {}, [0] * 6, {}

        def claim(pe, key, ring):
            n = turn.get(ring, 0)
            turn[ring] = n + 1
            t = Tile()
            u = ring[n % len(ring)]
            t.wide = pair[u] if u < 2 else None
            t.ap = pair[u][:, 0] if u < 2 else one[u - 2][:, :]
            t.filled, t.drained = filled[u], drained[u]
            if uses[u]:
                pe.wait_ge(t.drained, uses[u])
            uses[u] += 1
            t.nth = uses[u]
            assert key not in tiles, key
            tiles[key] = t
            return t

        ALL = (2, 3, 4, 5, 0, 1)

        x_in = [sem(f"x_in{b}") for b in range(B)]
        par_in = [sem(f"par_in{n}") for n in range(len(CHUNKS))]
        half_in = sem("half_in")
        ctx_in = sem("ctx_in")
        small_in = sem("small_in")
        presets = sem("presets")
        stats_ready = sem("stats_ready")
        rstd_ready = sem("rstd_ready")
        xn_ready = sem("xn_ready")
        res_ready = sem("res_ready")
        bias_ready = sem("bias_ready")
        max_ready = sem("max_ready")
        rinv_ready = sem("rinv_ready")
        out_done = sem("out_done")
        dve_step = sem("dve_step")
        pool_step = sem("pool_step")
        hi_ready = sem("hi_ready")
        lo_ready = sem("lo_ready")
        kadd_ready = sem("kadd_ready")
        mx_ready = sem("mx_ready")
        p_used = sem("p_used")
        vpast_ready = sem("vpast_ready")
        diff_ready = sem("diff_ready")
        e_ready = sem("e_ready")
        score_ready = sem("score_ready")
        g_ready = sem("g_ready")
        g_used = sem("g_used")
        rot_ready = sem("rot_ready")
        th_ready = sem("th_ready")
        vpad_ready = sem("vpad_ready")
        absd_ready = sem("absd_ready")
        off_used = sem("off_used")
        state_ready = sem("state_ready")
        rms_ready = sem("rms_ready")
        rms_pow = sem("rms_pow")
        turns_ready = sem("turns_ready")
        fold_ready = sem("fold_ready")
        phase_ready = sem("phase_ready")
        sinv_ready = sem("sinv_ready")
        wrap_ready = sem("wrap_ready")
        hi16_ready = sem("hi16_ready")
        kw_in = [sem(f"kw_in{n}") for n in range(KR)]
        ones_ready = sem("ones_ready")
        sine_ready = sem("sine_ready")
        act_ready = sem("act_ready")

        block = stack.enter_context(nc.Block())

        quads_used = []

        def residual_there(eng, l, b):
            if l == 0:
                eng.wait_ge(x_in[b], 16)
            elif l == 4:
                eng.wait_ge(res_ready, b + 1)
            else:
                t = tiles[("y", l - 1, b)]
                eng.wait_ge(t.drained, t.nth)

        def window(a, n):
            return a[:, (HD + 1) * n:(HD + 1) * n + 32]

        def used_diagonals(eng, j):
            t = tiles[("nt", j // B, j % B)]
            eng.wait_ge(t.filled, t.nth)

        def pair_keys(tag):
            return [(NC, KC, True)] if tag == "b" else [(n, 128, False) for n in range(NC)] + [(NC, KC, True)]

        @block.tensor
        def _(pe):
            def norm_T(l):
                for b in range(B):
                    pe.wait_ge(xn_ready, l * B + b + 1)
                    if l == 0 and b == 0:
                        pe.wait_ge(par_in[0], 16)
                    t = claim(pe, ("xT", l, b), ALL)
                    for c in range(NC):
                        mm = pe.transpose(t.ap[:, c * 128:(c + 1) * 128], xn[:, b, c, :], ident)
                    mm.then_inc(t.filled, 1)

            def feature_major(key, w, b, n=S, rhs=None):
                t = claim(pe, key, ALL)
                pe.matmul(t.ap[:, 0:n], w, xnT[:, b] if rhs is None else rhs, start=True, stop=True).then_inc(t.filled, 1)

            def token_major(key, lhs, w, wn=128):
                t = claim(pe, key, ALL)
                for c in range(NC):
                    mm = pe.matmul(t.ap[:, c * wn:(c + 1) * wn], lhs[:, c * 128:(c + 1) * 128], w, start=True, stop=True)
                mm.then_inc(t.filled, 1)

            def ready(key):
                t = tiles[key]
                pe.wait_ge(t.drained, t.nth)

            norm_T(0)
            for b in range(B):
                ready(("xT", 0, b))
                feature_major(("qT", 0, b), par_of("a_wq"), b)
                feature_major(("kT", 0, b), par_of("a_wk"), b)
                token_major(("v", 0, b), xnT[:, b], par_of("a_wv"))
            for b in range(B):
                ready(("qT", 0, b))
                ready(("kT", 0, b))
                for c in range(NC):
                    t = claim(pe, ("s", b, c), ALL)
                    pe.matmul(t.ap, qT[:, b, c * 128:(c + 1) * 128], kT[:, b], start=True, stop=True).then_inc(t.filled, 1)
            for b in range(B):
                ready(("v", 0, b))
                for c in range(NC):
                    t = claim(pe, ("pT", b, c), ALL)
                    ready(("s", b, c))
                    for k in range(NC):
                        mm = pe.transpose(t.ap[:, k * 128:(k + 1) * 128], big[:, b * NC + c, k * 128:(k + 1) * 128], ident)
                    mm.then_inc(t.filled, 1)
            for b in range(B):
                t = claim(pe, ("o", 0, b), ALL)
                for c in range(NC):
                    ready(("pT", b, c))
                    for k in range(NC):
                        mm = pe.matmul(t.ap[:, c * 128:(c + 1) * 128], PT[:, b * NC + c, k * 128:(k + 1) * 128],
                                       vtok[:, b, k], start=(k == 0), stop=(k == NC - 1))
                mm.then_inc(t.filled, 1)
            for b in range(B):
                ready(("o", 0, b))
                t = claim(pe, ("y", 0, b), ALL)
                for c in range(NC):
                    rows = Osb[:, b, c]
                    mm = pe.matmul(t.ap[:, c * 128:(c + 1) * 128], rows, par_of("a_wp"), start=True, stop=True)
                mm.then_inc(t.filled, 1)
            if LAST == 1:
                return

            def expand(key, which, b, s, n, at=0, col=0, t=None, first=True):
                src = slice(at, at + n)
                names = ("q_hi", "q_lo") if which == 0 else ("k_hi", "k_lo")
                o = t.ap[:, col:col + n]
                pe.matmul(o, half_of(names[0])[:, s * 128:(s + 1) * 128], hi[:, b, which, src], start=True, stop=False)
                return pe.matmul(o, half_of(names[1])[:, s * 128:(s + 1) * 128], lo[:, b, which, src], start=False, stop=True)

            def context_stack(tag, b):
                if tag == "b":
                    ready(("kT", 1, b))
                else:
                    pe.wait_ge(lo_ready, b + 1 + 2 * B)
                t = claim(pe, ("kc", tag, b), ALL)
                for s in range(SL):
                    mm = expand(None, 1, b, s, KC, at=S, col=s * KC, t=t)
                mm.then_inc(t.filled, 1)

            def stacks(tag, which, b):
                if tag == "d":
                    pe.wait_ge(lo_ready, 2 * b + which + 1)
                else:
                    ready((("qT", "kT")[which], {"b": 1, "e": 4}[tag], b))
                for s in range(SL):
                    t = claim(pe, ("st" + "qk"[which], tag, b, s), ALL)
                    expand(None, which, b, s, S, t=t).then_inc(t.filled, 1)

            def shift_T(tag, s, b, ring):
                if tag == "b":
                    ready(("mx", tag, s, b, NC - 1, -1))
                else:
                    pe.wait_ge(mx_ready, s * B + b + 1)
                t = claim(pe, ("mT", tag, s, b), ring)
                to = t.ap.bitcast(F16)
                for c in range(NC):
                    mm = pe.transpose(to[:, c * 128:(c + 1) * 128], Mx[:, b, s, c], ident16)
                mm.then_inc(t.filled, 1)

            def max_tile(tag, s, b, c, g, ring):
                t = claim(pe, ("mx", tag, s, b, c, g), ring)
                if g < 0:
                    pe.matmul(t.ap[:, 0:G * KC], qst[:, b, s, c * 128:(c + 1) * 128], kbd[:, b, s], start=True,
                              stop=True).then_inc(t.filled, 1)
                else:
                    pe.matmul(t.ap, qst[:, b, s, c * 128:(c + 1) * 128], kw[:, (s * B + b) % KR, g], start=True,
                              stop=True).then_inc(t.filled, 1)

            def score_tile(tag, s, b, k, nk, past, gp, first):
                if first:
                    ready(("mT", tag, s, b))
                t = claim(pe, ("sc", tag, s, b, k, gp), (0, 1))
                for i in range(2):
                    g = 2 * gp + i
                    keys = (kbd[:, b, s, g * KC:(g + 1) * KC] if past
                            else kw[:, (s * B + b) % KR, g, k * 128:(k + 1) * 128])
                    mm = pe.matmul(t.wide[0:nk, i], keys, qst[:, b, s], start=True, stop=True)
                mm.then_inc(t.filled, 1)

            def widened(j, tag):
                uses_before = (B * SL if tag == "e" else 0) + j
                pe.wait_ge(kw_in[j % KR], 64 * (uses_before // KR + 1))

            p_taken, early = [0], [0]

            def values(tag, s, b, k, nk, first, last):
                if first:
                    claim(pe, ("ov", tag, s, b), (5,))
                t = tiles[("ov", tag, s, b)]
                p_taken[0] += 2
                ready(("sc", tag, s, b, k, 1))
                for g in range(G):
                    buf = (p_taken[0] - 2 + g // 2) % 8
                    mm = pe.matmul(t.ap[32 * g:32 * g + 32], window(vst[0:nk, b, k], 4 * g + s),
                                   big[0:nk, 2 * buf + g % 2], start=first, stop=last)
                if last:
                    mm.then_inc(t.filled, 1)
                    quads_used.append((t.filled, t.nth))
                else:
                    mm.then_inc(p_used, 1)
                    early[0] += 1
                    quads_used.append((p_used, early[0]))

            def close(tag, b):
                for c in range(NC):
                    t = claim(pe, ("on", tag, b, c), ALL)
                    if c == 0:
                        for s in range(SL):
                            ready(("ov", tag, s, b))
                    for s in range(SL):
                        mm = pe.transpose(t.ap[:, s * 128:(s + 1) * 128], oT[:, b, s, c * 128:(c + 1) * 128], ident)
                    mm.then_inc(t.filled, 1)

            def project(tag, l, b, weights):
                t = claim(pe, ("onT", tag, b), ALL)
                for c in range(NC):
                    ready(("on", tag, b, c))
                    mm = pe.transpose(t.ap[:, c * 128:(c + 1) * 128], on[:, b, c], ident)
                mm.then_inc(t.filled, 1)
                ready(("onT", tag, b))
                token_major(("y", l, b), onT[:, b], weights)

            def cross_attention(l, tag):
                if tag == "b":
                    pe.wait_ge(par_in[1], 16)
                    pe.wait_ge(half_in, 16)
                    for b in range(B):
                        cT = par_of("ctxT")[:, b * KC:(b + 1) * KC]
                        feature_major(("kT", l, b), par_of("b_wk"), b, KC, cT)
                        t = claim(pe, ("v", l, b), ALL)
                        pe.matmul(t.ap[0:KC, 0:128], cT, par_of("b_wv"), start=True, stop=True).then_inc(t.filled, 1)
                    for b in range(B):
                        context_stack(tag, b)
                    norm_T(l)
                    for b in range(B):
                        ready(("xT", l, b))
                        feature_major(("qT", l, b), par_of("b_wq"), b)
                    for b in range(B):
                        stacks(tag, 0, b)
                else:
                    pe.wait_ge(par_in[6], 16)
                    for b in range(B):
                        context_stack(tag, b)
                    norm_T(l)
                    for b in range(B):
                        ready(("xT", l, b))
                        feature_major(("kT", l, b), par_of("e_wk"), b)
                        feature_major(("qT", l, b), par_of("e_wq"), b)
                        token_major(("v", l, b), xnT[:, b], par_of("e_wv"))
                    for b in range(B):
                        stacks(tag, 1, b)
                        stacks(tag, 0, b)
                ring = (2, 3, 4)
                items = [(s, b) for s in range(SL) for b in range(B)]
                keys = pair_keys(tag)

                def max_list(i):
                    s, b = items[i]
                    return [(tag, s, b, c, g) for c in range(NC) for g in ([-1] if tag == "b" else [0, 1, 2, 3, -1])]

                for b in range(B):
                    ready(("kc", tag, b))
                    for s in range(SL):
                        ready(("stq", tag, b, s))
                        if tag == "e":
                            ready(("stk", tag, b, s))
                for b in range(B):
                    ready(("v", l, b))
                for i in range(2):
                    if tag == "e":
                        widened(i, tag)
                    for m in max_list(i):
                        max_tile(*m, ring)
                shift_T(tag, *items[0], ring)
                for i, (s, b) in enumerate(items):
                    ahead = max_list(i + 2) if i + 2 < len(items) else []
                    if ahead and tag == "e":
                        widened(i + 2, tag)
                    halves_ = [(k, gp) for k in range(len(keys)) for gp in range(2)]
                    share = -(-len(ahead) // len(halves_))
                    for n, (k, gp) in enumerate(halves_):
                        kn, nk, past = keys[k]
                        score_tile(tag, s, b, kn, nk, past, gp, n == 0)
                        for m in ahead[n * share:(n + 1) * share]:
                            max_tile(*m, ring)
                        if n == 1 and i + 1 < len(items):
                            shift_T(tag, *items[i + 1], ring)
                        if gp == 1 and k >= 1:
                            kp = keys[k - 1]
                            values(tag, s, b, kp[0], kp[1], k == 1, False)
                    kp = keys[-1]
                    values(tag, s, b, kp[0], kp[1], len(keys) == 1, True)
                for b in range(B):
                    close(tag, b)
                for b in range(B):
                    project(tag, l, b, par_of("b_wp") if tag == "b" else par_of("e_wo"))

            cross_attention(1, "b")
            if LAST == 2:
                return

            norm_T(2)
            pe.wait_ge(par_in[2], 16)
            for b in range(B):
                ready(("xT", 2, b))
                token_major(("lg", b), xnT[:, b], par_of("c_wg"), NE)
            R4 = (0, 1, 2, 3)
            for b in range(B):
                pe.wait_ge(score_ready, b + 1)
                t = claim(pe, ("sT", b), R4)
                for c in range(NC):
                    mm = pe.transpose(t.ap[0:NE, c * 128:(c + 1) * 128], small[9][:, b, c], ident)
                mm.then_inc(t.filled, 1)
            yt = [claim(pe, ("y", 2, b), (4 + b,)) for b in range(B)]
            g_taken = [0]

            def down(e, b):
                for hf in range(2):
                    if hf == 0:
                        pe.wait_ge(g_ready, g_taken[0] // 2 + 1)
                    else:
                        ready(("sb", e, b))
                    buf = g_taken[0] % 8
                    g_taken[0] += 1
                    for c in range(NC):
                        mm = pe.matmul(yt[b].ap[:, c * 128:(c + 1) * 128], big[:, 8 + buf, c * 128:(c + 1) * 128],
                                       par_of("c_w2")[:, (2 * e + hf) * 128:(2 * e + hf + 1) * 128],
                                       start=(e == 0 and hf == 0 and c == 0), stop=False, skip_group_check=True)
                    mm.then_inc(g_used, 1)

            order = [(e, b) for e in range(NE) for b in range(B)]
            for b in range(B):
                ready(("sT", b))
            pe.wait_ge(par_in[3], 16)
            for i, (e, b) in enumerate(order):
                t = claim(pe, ("sb", e, b), R4)
                pe.matmul(t.ap, half_of("sel_e")[:, e * 128:(e + 1) * 128], s16[:, b], start=True,
                          stop=True).then_inc(t.filled, 1)
                for hf in range(2):
                    t = claim(pe, ("h", e, b, hf), R4)
                    w = par_of("c_w1")[:, e * FE + hf * 128:e * FE + (hf + 1) * 128]
                    pe.matmul(t.ap, w, xnT[:, b], start=True, stop=True).then_inc(t.filled, 1)
                if i >= 1:
                    down(*order[i - 1])
            down(*order[-1])
            for b in range(B):
                for c in range(NC):
                    mm = pe.matmul(yt[b].ap[:, c * 128:(c + 1) * 128], s32[:, b, c * 128:(c + 1) * 128],
                                   par_of("c_b2")[0:NE, :], start=False, stop=(c == NC - 1), skip_group_check=True)
                mm.then_inc(yt[b].filled, 1)
            if LAST == 3:
                return

            norm_T(3)
            pe.wait_ge(par_in[4], 16)
            pe.wait_ge(par_in[5], 16)
            for b in range(B):
                ready(("xT", 3, b))
                for n, w in enumerate(("d_wq", "d_wqs", "d_wk", "d_wks")):
                    feature_major(("r", b, n), par_of(w), b)
                token_major(("v", 3, b), xnT[:, b], par_of("d_wv"))
                token_major(("gate", b), xnT[:, b], par_of("d_wg"))
            for b in range(B):
                pe.wait_ge(rot_ready, 2 * b + 2)
                token_major(("ktok", b), rot[:, b, 1], ident)
                stacks("d", 0, b)
                stacks("d", 1, b)
            for b in range(B):
                ready(("ktok", b))
                ready(("v", 3, b))
                for c in range(NC - 1):
                    t = claim(pe, ("kv", b, c), ALL)
                    pe.matmul(t.ap[:, 0:128], ktok[:, b, c], vtok[:, b, c], start=True, stop=True).then_inc(t.filled, 1)
            for b in range(B):
                t = claim(pe, ("cr", b), ALL)
                for c in range(1, NC):
                    if c == 1:
                        ready(("kv", b, 0))
                    else:
                        pe.wait_ge(state_ready, b * (NC - 2) + c - 1)
                    mm = pe.matmul(t.ap[:, c * 128:(c + 1) * 128], rot[:, b, 0, c * 128:(c + 1) * 128],
                                   state[:, b, c - 1], start=True, stop=True)
                mm.then_inc(t.filled, 1)
            for b in range(B):
                for s in range(SL):
                    ready(("stq", "d", b, s))
                    ready(("stk", "d", b, s))
                pe.wait_ge(vpad_ready, b + 1)
            heads = [(s, b, g) for s in range(SL) for b in range(B) for g in range(G)]

            def ret_scores(s, b, g):
                keys = kw[:, (s * B + b) % KR, g]
                if g == 0:
                    widened(s * B + b, "d")
                t = claim(pe, ("dg", s, b, g), (2, 3, 4))
                for c in range(NC):
                    w = slice(c * 128, (c + 1) * 128)
                    mm = pe.matmul(t.ap[:, w], keys[:, w], qst[:, b, s, w], start=True, stop=True)
                mm.then_inc(t.filled, 1)
                t = claim(pe, ("of", s, b, g), (0, 1))
                pe.matmul(t.wide[:, 0, 0:384], keys[:, 0:128], qst[:, b, s, 128:512], start=True, stop=True)
                pe.matmul(t.wide[:, 0, 384:512], keys[:, 256:384], qst[:, b, s, 384:512], start=True, stop=True)
                pe.matmul(t.wide[:, 1, 0:256], keys[:, 128:256], qst[:, b, s, 256:512], start=True,
                          stop=True).then_inc(t.filled, 1)

            def ones_of(c):
                return par_of("d_one")[:, c * VW:(c + 1) * VW]

            def ret_sums(j):
                s, b = j // B, j % B
                t = claim(pe, ("nt", s, b), (5,))
                for g in range(G):
                    ready(("of", s, b, g))
                    A = Aoff[g]
                    o = t.ap[32 * g:32 * g + 32]
                    wa = [window(ones_of(c), 4 * g + s) for c in range(3)]
                    pe.matmul(o[:, 128:512], wa[0], A[:, 0:384], start=True, stop=False, skip_group_check=True)
                    pe.matmul(o[:, 384:512], wa[2], A[:, 384:512], start=False, stop=False, skip_group_check=True)
                    pe.matmul(o[:, 256:512], wa[1], A[:, 512:768], start=False, stop=False,
                              skip_group_check=True).then_inc(off_used, 1)
                pe.wait_ge(absd_ready, 4 * j + 4)
                for c in range(NC):
                    w = slice(c * 128, (c + 1) * 128)
                    for g in range(G):
                        pe.matmul(t.ap[32 * g:32 * g + 32, w], window(ones_of(c), 4 * g + s),
                                  big[:, 8 + (4 * j + g) % 8, w], start=False, stop=False, skip_group_check=True)
                    for g in range(G):
                        mm = pe.matmul(t.ap[32 * g:32 * g + 32, w], window(vst[:, b, c], 4 * g + s), big[:, (4 * j + g) % 8, w],
                                       start=False, stop=(c == NC - 1), skip_group_check=True)
                mm.then_inc(t.filled, 1)

            for n, (s, b, g) in enumerate(heads):
                ret_scores(s, b, g)
                if n % 4 == 1 and n >= 4:
                    ret_sums(n // 4 - 1)
            ret_sums(len(heads) // 4 - 1)
            for b in range(B):
                for c in range(NC):
                    t = claim(pe, ("nq", b, c), ALL)
                    if c == 0:
                        for s in range(SL):
                            ready(("nt", s, b))
                    for s in range(SL):
                        mm = pe.transpose(t.ap[:, s * 128:(s + 1) * 128], oT[:, b, s, c * 128:(c + 1) * 128], ident)
                    mm.then_inc(t.filled, 1)
            if LAST == 4:
                return

            cross_attention(4, "e")
            if LAST == 5:
                return

            norm_T(5)
            for b in range(B):
                ready(("xT", 5, b))
            for b in range(B):
                for j in range(NJ):
                    feature_major(("f1", b, j), par_of("f_w1")[:, j * 128:(j + 1) * 128], b)
            for b in range(B):
                t = claim(pe, ("y", 5, b), ALL)
                pe.wait_ge(act_ready, b * NJ + NJ)
                for c in range(NC):
                    for j in range(NJ):
                        mm = pe.matmul(t.ap[:, c * 128:(c + 1) * 128], big[:, 8 + b * NJ + j, c * 128:(c + 1) * 128],
                                       par_of("f_w2")[:, j * 128:(j + 1) * 128], start=(j == 0), stop=(j == NJ - 1))
                mm.then_inc(t.filled, 1)

        @block.vector
        def _(dve):
            steps = [0]

            def link(ins):
                steps[0] += 1
                ins.then_inc(dve_step, 1)
                dve.wait_ge(dve_step, steps[0])

            def full(key):
                t = tiles[key]
                dve.wait_ge(t.filled, t.nth)
                return t

            def ready(key):
                t = tiles[key]
                dve.wait_ge(t.drained, t.nth)

            v = nc.vector

            def norm(l):
                for b in range(B):
                    residual_there(dve, l, b)
                    for c in range(NC):
                        ins = v.bn_stats(bn[:, b, c], X[:, b, c])
                    link(ins)
                    for c in range(NC):
                        ins = v.bn_aggr(mv[:, b, c], bn[:, b, c])
                    ins.then_inc(stats_ready, 1)
                for b in range(B):
                    dve.wait_ge(rstd_ready, l * B + b + 1)
                    dve.wait_ge(stats_ready, l * B + b + 1)
                    for c in range(NC):
                        ins = v.tensor_scalar(xn[:, b, c], X[:, b, c], mv[:, b, c, 0:1], rstd[:, b, c:c + 1],
                                              ALU.subtract, ALU.mult)
                    ins.then_inc(xn_ready, 1)

            def residual(l, key, b, biased):
                t = full(key)
                if biased:
                    dve.wait_ge(bias_ready, biased * B - B + b + 1)
                v.tensor_tensor(X[:, b].rearrange("p c d -> p (c d)"), t.ap,
                                (R if biased else X)[:, b].rearrange("p c d -> p (c d)"), ALU.add).then_inc(t.drained, 1)

            norm(0)
            for b in range(B):
                t = full(("kT", 0, b))
                v.tensor_copy(kT[:, b], t.ap).then_inc(t.drained, 1)
            for b in range(B):
                for c in range(NC):
                    t = full(("s", b, c))
                    v.tensor_reduce(negmax[:, b, c:c + 1], t.ap, AX.X, ALU.max, negate=True).then_inc(max_ready, 1)
            for b in range(B):
                ready(("s", b, NC - 1))
                v.reciprocal(rinv[:, b], rowsum[:, b]).then_inc(rinv_ready, 1)
                for c in range(0, NC, 2):
                    t = full(("pT", b, c))
                    v.tensor_copy(PT[:, b * NC + c], t.ap).then_inc(t.drained, 1)
            for b in range(B):
                t = full(("o", 0, b))
                dve.wait_ge(rinv_ready, b + 1)
                v.tensor_tensor(Osb[:, b].rearrange("p c d -> p (c d)").rearrange("p (d j) -> p j d", j=NC), t.ap.rearrange("p (c d) -> p c d", c=NC),
                                rinv[:, b].unsqueeze(2).to_broadcast([128, NC, 128]), ALU.mult).then_inc(t.drained, 1)
            for b in range(B):
                residual(0, ("y", 0, b), b, 1)
            if LAST == 1:
                return

            def low_part(b, which, at, key, src, bias, n_hi):
                dve.wait_ge(hi_ready, n_hi)
                ins = v.scalar_tensor_tensor(out=lo[:, b, which, at], in0=src, scalar=bias, in1=hi[:, b, which, at],
                                             op0=ALU.add, op1=ALU.subtract)
                if key:
                    ins.then_inc(tiles[key].drained, 1)
                else:
                    ins.then_inc(lo_ready, 1)

            def context_rows(tag, b):
                t = full(("kc", tag, b))
                for g in range(G):
                    r = slice(32 * g, 32 * g + 32)
                    ins = v.tensor_tensor(kbd[r, b, :, g * KC:(g + 1) * KC],
                                          t.ap[r, 0:SL * KC].rearrange("p (s k) -> p s k", s=SL),
                                          kadd[r, b].unsqueeze(1).to_broadcast([32, SL, KC]), ALU.add)
                ins.then_inc(t.drained, 1)

            def maxima(tag, s, b, i, items, shift_at):
                groups = [-1] if tag == "b" else [0, 1, 2, 3, -1]
                n = 0
                for c in range(NC):
                    for g in groups:
                        t = full(("mx", tag, s, b, c, g))
                        if g < 0:
                            src = t.ap[:, 0:G * KC].rearrange("p (g k) -> p g k", g=G)
                            dst = (Mx[:, b, s, c].rearrange("p (g j) -> p g j", g=G)[:, :, 0] if tag == "b"
                                   else Mp[:, b, c * G:(c + 1) * G])
                        else:
                            src = t.ap
                            dst = Mn[:, b, c * G + g:c * G + g + 1]
                        ins = v.tensor_reduce(dst, src, AX.X, ALU.max)
                        ins.then_inc(t.drained, 1)
                        n += 1
                        if shift_at is not None and n == 3:
                            shift(tag, *items[shift_at])
                if tag == "e":
                    for g in groups:
                        ready(("mx", tag, s, b, NC - 1, g))
                    v.tensor_tensor(Mx[:, b, s].rearrange("p c (g j) -> p c g j", g=G)[:, :, :, 0],
                                    Mp[:, b].rearrange("p (c g) -> p c g", c=NC),
                                    Mn[:, b].rearrange("p (c g) -> p c g", c=NC), ALU.max).then_inc(mx_ready, 1)

            def shift(tag, s, b):
                t = full(("mT", tag, s, b))
                v.tensor_tensor(qst[:, b, s], t.ap.bitcast(F16)[:, 0:S], qst[:, b, s], ALU.add).then_inc(t.drained, 1)

            def cross_attention(l, tag):
                if tag == "b":
                    dve.wait_ge(par_in[1], 16)
                    dve.wait_ge(small_in, 32)
                    dve.wait_ge(presets, 1)
                    for b in range(B):
                        v.tensor_scalar(kadd[:, b], mask_u[:, b], par_of("kmask"), par_of("kconst"), ALU.mult,
                                        ALU.add).then_inc(kadd_ready, 1)
                    for b in range(B):
                        low_part(b, 1, slice(S, PK), ("kT", l, b), tiles[("kT", l, b)].ap[:, 0:KC], par_of("b_kb"), b + 1)
                        t = full(("v", l, b))
                        v.tensor_tensor(vhead[0:KC, b, NC, :, 0:HD], t.ap[0:KC, 0:128].rearrange("p (h d) -> p h d", h=H),
                                        par_of("b_vb")[0:KC].rearrange("p (h d) -> p h d", h=H), ALU.add).then_inc(t.drained, 1)
                    dve.wait_ge(kadd_ready, B)
                    for b in range(B):
                        context_rows(tag, b)
                    norm(l)
                    for b in range(B):
                        low_part(b, 0, slice(0, S), ("qT", l, b), tiles[("qT", l, b)].ap, par_of("b_qb"), B + b + 1)
                else:
                    dve.wait_ge(ctx_in, 16)
                    link(v.tensor_copy(lens_f[:, :], lens_i[:, :]))
                    link(v.tensor_tensor(maxlen[:, :], lens_f[:, 0:1], lens_f[:, 1:2], ALU.max))
                    for b in range(B):
                        v.tensor_scalar(posm[:, b], par_of("posrow"), lens_f[:, b:b + 1], None, ALU.is_lt)
                        v.tensor_scalar(kpast[:, b], par_of("posrow"), maxlen[:, 0:1], par_of("kmask"), ALU.is_ge, ALU.mult)
                        link(v.tensor_scalar(vkeep[:, b:b + 1], par_of("pos"), lens_f[:, b:b + 1], None, ALU.is_lt))
                        v.tensor_scalar(kadd[:, b], kpast[:, b], par_of("kconst"), None, ALU.add).then_inc(kadd_ready, 1)
                        v.tensor_scalar(vhead[0:KC, b, NC, :, 0:HD], ctxk[:, b].rearrange("p (h d) -> p h d", h=H),
                                        vkeep[0:KC, b:b + 1], None, ALU.mult).then_inc(vpast_ready, 1)
                    dve.wait_ge(kadd_ready, 2 * B)
                    for b in range(B):
                        v.tensor_tensor(kpast[:, b], par_of("ctxT")[:, b * KC:(b + 1) * KC], posm[:, b],
                                        ALU.mult).then_inc(kadd_ready, 1)
                    for b in range(B):
                        dve.wait_ge(kadd_ready, 2 * B + b + 1)
                        low_part(b, 1, slice(S, PK), None, kpast[:, b], 0.0, 4 * B + b + 1)
                    for b in range(B):
                        context_rows(tag, b)
                    norm(l)
                    for b in range(B):
                        for which, name in ((1, "kT"), (0, "qT")):
                            low_part(b, which, slice(0, S), (name, l, b), tiles[(name, l, b)].ap, 0.0,
                                     5 * B + 2 * b + (2 - which))
                items = [(s, b) for s in range(SL) for b in range(B)]
                for i in range(2):
                    maxima(tag, *items[i], i, items, None)
                for b in range(B):
                    for s in range(SL):
                        ready(("stq", tag, b, s))
                shift(tag, *items[0])
                for i in range(len(items)):
                    if i + 2 < len(items):
                        maxima(tag, *items[i + 2], i, items, i + 1)
                    elif i + 1 < len(items):
                        shift(tag, *items[i + 1])
                for b in range(B):
                    for c in range(NC):
                        t = full(("on", tag, b, c))
                        ps = t.ap.rearrange("p (s g j) -> p s g j", s=SL, g=G)
                        link(v.reciprocal(rden[:, b, c], ps[:, :, :, HD]))
                        o = on[:, b, c].rearrange("p (g s d) -> p s g d", g=G, s=SL)
                        v.tensor_tensor(o, ps[:, :, :, 0:HD], rden[:, b, c].unsqueeze(3).to_broadcast([128, SL, G, HD]),
                                        ALU.mult).then_inc(t.drained, 1)
                for b in range(B):
                    residual(l, ("y", l, b), b, {"b": 2, "e": 3}[tag])

            cross_attention(1, "b")
            if LAST == 2:
                return

            norm(2)
            lg, top, gt, eq, run, sel, ex, w, df, sc = small
            n_gt, wsum, winv = thin
            for b in range(B):
                t = full(("lg", b))
                v.tensor_copy(lg[:, b], t.ap[:, 0:NC * NE].rearrange("p (c e) -> p c e", c=NC)).then_inc(t.drained, 1)
            for b in range(B):
                ready(("lg", b))
                for c in range(NC):
                    ins = v.max(top[:, b, c], lg[:, b, c])
                link(ins)
                best = top[:, b, :, 0:1].to_broadcast([128, NC, NE])
                second = top[:, b, :, 1:2].to_broadcast([128, NC, NE])
                v.tensor_tensor(df[:, b], lg[:, b], best, ALU.subtract).then_inc(diff_ready, 1)
                v.tensor_tensor(gt[:, b], lg[:, b], second, ALU.is_gt)
                link(v.tensor_tensor(eq[:, b], lg[:, b], second, ALU.is_equal))
                v.tensor_reduce(n_gt[:, b], gt[:, b], AX.X, ALU.add)
                link(v.tensor_tensor_scan(run[:, b].rearrange("p c e -> p (c e)"), par_of("c_reset"),
                                          eq[:, b].rearrange("p c e -> p (c e)"), 0.0, ALU.mult, ALU.add))
                link(v.tensor_tensor(run[:, b], run[:, b], n_gt[:, b].unsqueeze(2).to_broadcast([128, NC, NE]), ALU.add))
                link(v.scalar_tensor_tensor(out=sel[:, b], in0=run[:, b], scalar=2.0, in1=eq[:, b], op0=ALU.is_le,
                                            op1=ALU.mult))
                link(v.tensor_tensor(sel[:, b], sel[:, b], gt[:, b], ALU.add))
                dve.wait_ge(e_ready, b + 1)
                link(v.tensor_tensor(w[:, b], ex[:, b], sel[:, b], ALU.mult))
                link(v.tensor_reduce(wsum[:, b], w[:, b], AX.X, ALU.add))
                link(v.reciprocal(winv[:, b], wsum[:, b]))
                v.tensor_tensor(sc[:, b], w[:, b], winv[:, b].unsqueeze(2).to_broadcast([128, NC, NE]),
                                ALU.mult).then_inc(score_ready, 1)
            for b in range(B):
                t = full(("sT", b))
                dve.wait_ge(hi16_ready, b + 1)
                v.tensor_tensor(s16[32:32 + NE, b], t.ap[0:NE], s16[0:NE, b], ALU.subtract).then_inc(t.drained, 1)
            n = 0
            for e in range(NE):
                for b in range(B):
                    t = full(("sb", e, b))
                    for hf in range(2):
                        ready(("h", e, b, hf))
                        if n >= 8:
                            dve.wait_ge(g_used, n - 7)
                        ins = v.tensor_tensor(big[:, 8 + n % 8], t.ap, big[:, n % 8], ALU.mult)
                        ins.then_inc(g_ready if hf == 0 else t.drained, 1)
                        n += 1
            for b in range(B):
                residual(2, ("y", 2, b), b, 0)
            if LAST == 3:
                return

            norm(3)
            dve.wait_ge(par_in[4], 16)
            dve.wait_ge(par_in[5], 16)
            for b in range(B):
                for which, (cn, sn) in enumerate((("d_cosq", "d_sinq"), ("d_cosk", "d_sink"))):
                    t = full(("r", b, 2 * which))
                    rt1, rt2 = big[:, 4 * b + 2 * which], big[:, 4 * b + 2 * which + 1]
                    v.tensor_tensor(rt1, t.ap, par_of(cn), ALU.mult).then_inc(t.drained, 1)
                    u = full(("r", b, 2 * which + 1))
                    v.tensor_tensor(rt2, u.ap, par_of(sn), ALU.mult).then_inc(u.drained, 1)
                    dve.wait_ge(t.drained, t.nth)
                    dve.wait_ge(u.drained, u.nth)
                    v.tensor_tensor(rot[:, b, which], rt1, rt2, ALU.add).then_inc(rot_ready, 1)
                t = full(("gate", b))
                dve.wait_ge(th_ready, b + 1)
                v.scalar_tensor_tensor(out=th[:, b].rearrange("p c d -> p (c d)"),
                                       in0=th[:, b].rearrange("p c d -> p (c d)"), scalar=1.0, in1=t.ap, op0=ALU.add,
                                       op1=ALU.mult).then_inc(t.drained, 1)
            for b in range(B):
                for which in range(2):
                    dve.wait_ge(hi_ready, 2 * B + 2 * b + which + 1)
                    dve.wait_ge(rot_ready, 2 * b + which + 1)
                    v.tensor_tensor(lo[:, b, which, 0:S], rot[:, b, which], hi[:, b, which, 0:S],
                                    ALU.subtract).then_inc(lo_ready, 1)
            for b in range(B):
                for c in range(NC - 1):
                    t = full(("kv", b, c))
                    if c == 0:
                        v.tensor_tensor(state[:, b, 0], t.ap[:, 0:128], par_of("d_gm"), ALU.mult).then_inc(t.drained, 1)
                    else:
                        if c == 1:
                            ready(("kv", b, 0))
                        else:
                            dve.wait_ge(state_ready, b * (NC - 2) + c - 1)
                        v.tensor_tensor(stmp[:, b], t.ap[:, 0:128], state[:, b, c - 1], ALU.add).then_inc(t.drained, 1)
                        dve.wait_ge(t.drained, t.nth)
                        v.tensor_tensor(state[:, b, c], stmp[:, b], par_of("d_gm"), ALU.mult).then_inc(state_ready, 1)
            for n in range(B * H):
                s, b, g = n // (B * G), n // G % B, n % G
                t = full(("dg", s, b, g))
                if n >= 8:
                    used_diagonals(dve, n // 4 - 2)
                v.tensor_tensor(big[:, n % 8].rearrange("p (c q) -> p c q", c=NC), t.ap.rearrange("p (c q) -> p c q", c=NC),
                                par_of("d_tri").unsqueeze(1).to_broadcast([128, NC, 128]), ALU.mult).then_inc(t.drained, 1)
                if n % 3 != 0:
                    t = full(("of", s, b, g))
                    if n >= 4:
                        dve.wait_ge(off_used, n - 3)
                    v.tensor_scalar(Aoff[n % 4].bitcast(I32), t.wide.rearrange("p a q -> p (a q)")[:, 0:768].bitcast(I32),
                                    0x7FFFFFFF, None, ALU.bitwise_and).then_inc(t.drained, 1)
            dens, fac, ss, rr, tmp, fin = f16h
            num = xn
            sq = on
            for b in range(B):
                ready(("cr", b))
                for c in range(NC):
                    t = full(("nq", b, c))
                    ps = t.ap.rearrange("p (s g j) -> p s g j", s=SL, g=G)
                    v.tensor_copy(dens[:, b, c * H:(c + 1) * H].rearrange("p (s g) -> p s g", s=SL), ps[:, :, :, HD])
                    perm = "p (g s d) -> p s g d"
                    to = num[:, b, c].rearrange(perm, g=G, s=SL)
                    if c == 0:
                        v.tensor_copy(to, ps[:, :, :, 0:HD]).then_inc(t.drained, 1)
                    else:
                        v.tensor_tensor(to, ps[:, :, :, 0:HD], cross[:, b, c].rearrange(perm, g=G, s=SL),
                                        ALU.add).then_inc(t.drained, 1)
                ready(("nq", b, NC - 1))
                for c in range(NC - 1):
                    ready(("nq", b, c))
                flat = lambda a: a[:, b].rearrange("p c d -> p (c d)")
                v.tensor_tensor(flat(sq), flat(num), flat(num), ALU.mult)
                link(v.tensor_tensor(dens[:, b], dens[:, b], par_of("d_td"), ALU.mult))
                link(v.tensor_scalar(dens[:, b], dens[:, b], 1.0, 50000.0, ALU.max, ALU.min))
                link(v.reciprocal(rr[:, b], dens[:, b]))
                link(v.tensor_tensor(fac[:, b], rr[:, b], par_of("d_tn"), ALU.mult))
                for c in range(NC):
                    ins = v.tensor_reduce(ss[:, b, c * H:(c + 1) * H].rearrange("p (s g) -> p s g", s=SL),
                                          sq[:, b, c].rearrange("p (g s d) -> p s g d", g=G, s=SL), AX.X, ALU.add)
                link(ins)
                link(v.tensor_tensor(tmp[:, b], fac[:, b], fac[:, b], ALU.mult))
                link(v.tensor_tensor(ss[:, b], ss[:, b], tmp[:, b], ALU.mult))
                v.tensor_scalar(ss[:, b], ss[:, b], 1.0 / HD, RMS_EPS, ALU.mult, ALU.add).then_inc(rms_ready, 1)
            for b in range(B):
                dve.wait_ge(rms_pow, b + 1)
                link(v.scalar_tensor_tensor(out=fin[:, b], in0=fin[:, b], scalar=0.5, in1=fac[:, b], op0=ALU.mult,
                                            op1=ALU.mult))
                flat = lambda a: a[:, b].rearrange("p c d -> p (c d)")
                ready(("gate", b))
                link(v.tensor_tensor(flat(th), flat(th), flat(num), ALU.mult))
                for c in range(NC):
                    perm = "p (g s d) -> p s g d"
                    ins = v.tensor_tensor(th[:, b, c].rearrange(perm, g=G, s=SL), th[:, b, c].rearrange(perm, g=G, s=SL),
                                          fin[:, b, c * H:(c + 1) * H].rearrange("p (s g) -> p s g", s=SL).unsqueeze(3)
                                          .to_broadcast([128, SL, G, HD]), ALU.mult)
                link(ins)
                v.tensor_tensor(flat(X), flat(X), flat(th), ALU.add).then_inc(res_ready, 1)
            if LAST == 4:
                return

            cross_attention(4, "e")
            if LAST == 5:
                return

            dve.wait_ge(par_in[6], 16)
            n0, fold, absr, cosn, phs, amp, a1, a2 = tv[:8]
            link(v.tensor_scalar(n0[:, :], par_of("f_th"), 1.0 / TWO_PI, ROUND, ALU.mult, ALU.add))
            link(v.tensor_scalar(n0[:, :], n0[:, :], -ROUND, None, ALU.add))
            link(v.scalar_tensor_tensor(out=fold[:, :], in0=n0[:, :], scalar=-PI_A, in1=par_of("f_th"), op0=ALU.mult, op1=ALU.add))
            link(v.scalar_tensor_tensor(out=fold[:, :], in0=n0[:, :], scalar=-PI_B, in1=fold[:, :], op0=ALU.mult, op1=ALU.add))
            link(v.scalar_tensor_tensor(out=fold[:, :], in0=n0[:, :], scalar=-PI_C, in1=fold[:, :], op0=ALU.mult, op1=ALU.add))
            link(v.tensor_scalar(fold[:, :], fold[:, :], float(TURN / 2), -float(TURN / 2), ALU.min, ALU.max))
            link(v.scalar_tensor_tensor(out=absr[:, :], in0=fold[:, :], scalar=-1.0, in1=fold[:, :], op0=ALU.mult, op1=ALU.max))
            v.tensor_scalar(cosn[:, :], absr[:, :], -1.0, np.pi / 2, ALU.mult, ALU.add).then_inc(fold_ready, 1)
            link(v.tensor_scalar(phs[:, :], fold[:, :], 1.0 / TWO_PI, None, ALU.mult))
            v.scalar_tensor_tensor(out=phs[:, :], in0=par_of("f_b1"), scalar=0.1 / TWO_PI, in1=phs[:, :], op0=ALU.mult,
                                   op1=ALU.add).then_inc(phase_ready, 1)
            norm(5)
            dve.wait_ge(sinv_ready, 1)
            sin_v, cos_v = tv[8], tv[9]
            v.tensor_tensor(a1[:, :], cos_v[:, :], par_of("f_wr"), ALU.mult)
            link(v.tensor_tensor(a2[:, :], sin_v[:, :], par_of("f_wi"), ALU.mult))
            link(v.tensor_tensor(a1[:, :], a1[:, :], a2[:, :], ALU.add))
            link(v.scalar_tensor_tensor(out=amp[:, :], in0=a1[:, :], scalar=0.1, in1=par_of("f_wi"), op0=ALU.mult, op1=ALU.mult))

            def wrap(m):
                dve.wait_ge(turns_ready, m + 1)
                link(v.tensor_scalar(PT[:, m % 4], big[:, m], ROUND, None, ALU.add))
                v.scalar_tensor_tensor(out=PT[:, 4 + m % 4], in0=PT[:, m % 4], scalar=-ROUND, in1=big[:, m], op0=ALU.add,
                                       op1=ALU.subtract).then_inc(wrap_ready, 1)

            def mix(m):
                t = full(("f1", m // NJ, m % NJ))
                dve.wait_ge(sine_ready, m + 1)
                v.scalar_tensor_tensor(out=big[:, m], in0=big[:, m], scalar=amp[:, m % NJ:m % NJ + 1], in1=t.ap,
                                       op0=ALU.mult, op1=ALU.add).then_inc(t.drained, 1)

            for m in range(B * NJ + 1):
                if m < B * NJ:
                    wrap(m)
                if m >= 1:
                    mix(m - 1)
            for b in range(B):
                residual(5, ("y", 5, b), b, 4)

        @block.scalar
        def _(act):
            a = nc.scalar

            def full(key):
                t = tiles[key]
                act.wait_ge(t.filled, t.nth)
                return t

            def ready(key):
                t = tiles[key]
                act.wait_ge(t.drained, t.nth)

            def evac(key, dst, n=S, scale=1.0, bias=0.0, func=None):
                t = full(key)
                a.activation(dst, t.ap[:, 0:n], ACT.Identity, bias=bias, scale=scale).then_inc(t.drained, 1)

            def norm_T(l):
                for b in range(B):
                    evac(("xT", l, b), xnT[:, b])

            norm_T(0)
            for b in range(B):
                evac(("qT", 0, b), qT[:, b], scale=SCALE)
                evac(("v", 0, b), vtok[:, b].rearrange("p c d -> p (c d)"))
            for b in range(B):
                for c in range(NC):
                    t = full(("s", b, c))
                    act.wait_ge(max_ready, b * NC + c + 1)
                    a.activation(big[:, b * NC + c], t.ap, ACT.Exp, bias=negmax[:, b, c:c + 1],
                                 accum_out=rowsum[:, b, c:c + 1]).then_inc(t.drained, 1)
            for b in range(B):
                for c in range(1, NC, 2):
                    evac(("pT", b, c), PT[:, b * NC + c])
            if LAST == 1:
                return

            nb = [0]

            def high(key, dst, src, bias):
                if key:
                    full(key)
                a.activation(dst, src, ACT.Identity, bias=bias).then_inc(hi_ready, 1)

            def cross_attention(l, tag):
                if tag == "b":
                    act.wait_ge(par_in[1], 16)
                    act.wait_ge(presets, 1)
                    for b in range(B):
                        high(("kT", l, b), hi[:, b, 1, S:PK], tiles[("kT", l, b)].ap[:, 0:KC], par_of("b_kb"))
                    norm_T(l)
                    for b in range(B):
                        high(("qT", l, b), hi[:, b, 0, 0:S], tiles[("qT", l, b)].ap, par_of("b_qb"))
                else:
                    for b in range(B):
                        act.wait_ge(kadd_ready, 2 * B + b + 1)
                        high(None, hi[:, b, 1, S:PK], kpast[:, b], 0.0)
                    norm_T(l)
                    for b in range(B):
                        high(("kT", l, b), hi[:, b, 1, 0:S], tiles[("kT", l, b)].ap, 0.0)
                        high(("qT", l, b), hi[:, b, 0, 0:S], tiles[("qT", l, b)].ap, 0.0)
                        t = full(("v", l, b))
                        a.activation(vhead[:, b, 0:NC, :, 0:HD],
                                     t.ap.rearrange("p (c h d) -> p c h d", c=NC, d=HD), ACT.Identity).then_inc(t.drained, 1)
                for b in range(B):
                    for s in range(SL):
                        if tag == "e":
                            evac(("stk", tag, b, s), kst[:, b, s], bias=par_of("kconst"))
                    for s in range(SL):
                        evac(("stq", tag, b, s), qst[:, b, s], bias=par_of("qconst"))
                keys = pair_keys(tag)
                for i in range(SL * B):
                    s, b = i // B, i % B
                    for k, nk, past in keys:
                        for gp in range(2):
                            t = full(("sc", tag, s, b, k, gp))
                            if nb[0] >= 8:
                                act.wait_ge(*quads_used[nb[0] // 2 - 4])
                            buf = nb[0] % 8
                            a.activation(big[0:nk, 2 * buf:2 * buf + 2], t.wide[0:nk], ACT.Exp, scale=SCALE).then_inc(t.drained, 1)
                            nb[0] += 1
                    evac(("ov", tag, s, b), oT[:, b, s])
                for b in range(B):
                    evac(("onT", tag, b), onT[:, b])

            cross_attention(1, "b")
            if LAST == 2:
                return

            norm_T(2)
            for b in range(B):
                act.wait_ge(diff_ready, b + 1)
                a.activation(small[6][:, b], small[8][:, b], ACT.Exp).then_inc(e_ready, 1)
            for b in range(B):
                t = full(("sT", b))
                a.activation(s32[:, b], t.ap[0:NE], ACT.Identity)
                a.activation(s16[0:NE, b], t.ap[0:NE], ACT.Identity).then_inc(hi16_ready, 1)
            n = 0
            for e in range(NE):
                for b in range(B):
                    for hf in range(2):
                        t = full(("h", e, b, hf))
                        if n >= 8 and hf == 0:
                            eb = (n - 8) // 2
                            ready(("sb", eb // B, eb % B))
                        a.activation(big[:, n % 8], t.ap, ACT.Relu,
                                     bias=par_of("c_b1")[:, 2 * e + hf:2 * e + hf + 1]).then_inc(t.drained, 1)
                        n += 1
            if LAST == 3:
                return

            norm_T(3)
            for b in range(B):
                evac(("v", 3, b), vtok[:, b].rearrange("p c d -> p (c d)"))
                t = full(("gate", b))
                a.activation(th[:, b].rearrange("p c d -> p (c d)"), t.ap, ACT.Tanh, scale=0.5).then_inc(th_ready, 1)
                for which in range(2):
                    act.wait_ge(rot_ready, 2 * b + which + 1)
                    a.activation(hi[:, b, which, 0:S], rot[:, b, which], ACT.Identity).then_inc(hi_ready, 1)
            for b in range(B):
                evac(("ktok", b), ktok[:, b].rearrange("p c d -> p (c d)"))
                for s in range(SL):
                    evac(("stq", "d", b, s), qst[:, b, s])
                for s in range(SL):
                    evac(("stk", "d", b, s), kst[:, b, s])
            for b in range(B):
                t = full(("cr", b))
                act.wait_ge(presets, 1)
                a.activation(cross[:, b, 1:NC].rearrange("p c d -> p (c d)"), t.ap[:, 128:512],
                             ACT.Identity).then_inc(t.drained, 1)
            for n in range(B * H):
                s, b, g = n // (B * G), n // G % B, n % G
                ready(("dg", s, b, g))
                if n >= 8:
                    used_diagonals(act, n // 4 - 2)
                a.activation(big[:, 8 + n % 8], big[:, n % 8], ACT.Abs).then_inc(absd_ready, 1)
                if n % 3 == 0:
                    t = full(("of", s, b, g))
                    if n >= 4:
                        act.wait_ge(off_used, n - 3)
                    a.activation(Aoff[n % 4], t.wide.rearrange("p a q -> p (a q)")[:, 0:768], ACT.Abs).then_inc(t.drained, 1)
                if n % 4 == 3 and n >= 7:
                    i = n // 4 - 1
                    evac(("nt", i // B, i % B), oT[:, i % B, i // B])
            evac(("nt", SL - 1, B - 1), oT[:, B - 1, SL - 1])
            if LAST == 4:
                return

            cross_attention(4, "e")
            if LAST == 5:
                return

            norm_T(5)
            act.wait_ge(fold_ready, 1)
            a.activation(tv[8][:, :], tv[1][:, :], ACT.Sin)
            a.activation(tv[9][:, :], tv[3][:, :], ACT.Sin).then_inc(sinv_ready, 1)
            act.wait_ge(phase_ready, 1)

            def turns(m):
                t = full(("f1", m // NJ, m % NJ))
                a.activation(big[:, m], t.ap, ACT.Identity, bias=tv[4][:, m % NJ:m % NJ + 1],
                             scale=0.1 / TWO_PI).then_inc(turns_ready, 1)

            def sine(m):
                act.wait_ge(wrap_ready, m + 1)
                a.activation(big[:, m], PT[:, 4 + m % 4], ACT.Sin, scale=-TURN).then_inc(sine_ready, 1)

            def relu(m):
                ready(("f1", m // NJ, m % NJ))
                a.activation(big[:, 8 + m], big[:, m], ACT.Relu, bias=par_of("f_b1")[:, m % NJ:m % NJ + 1]).then_inc(act_ready, 1)

            for m in range(B * NJ + 2):
                if m < B * NJ:
                    turns(m)
                if 1 <= m <= B * NJ:
                    sine(m - 1)
                if m >= 2:
                    relu(m - 2)

        @block.gpsimd
        def _(pool):
            p = nc.gpsimd
            steps = [0]

            def link(ins):
                steps[0] += 1
                ins.then_inc(pool_step, 1)
                pool.wait_ge(pool_step, steps[0])

            link(p.memset(neghalf[:, :], -0.5))

            def norm(l, bias):
                for b in range(B):
                    pool.wait_ge(stats_ready, l * B + b + 1)
                    link(p.tensor_scalar(veps[:, b], mv[:, b, :, 1], LN_EPS, None, ALU.add))
                    p.tensor_tensor(rstd[:, b], veps[:, b], neghalf[:, 0:NC], ALU.pow).then_inc(rstd_ready, 1)
                if bias:
                    for b in range(B):
                        p.tensor_tensor(R[:, b], X[:, b], par_of(bias).unsqueeze(1).to_broadcast([128, NC, 128]),
                                        ALU.add).then_inc(bias_ready, 1)

            pool.wait_ge(par_in[0], 16)
            norm(0, "a_bp")
            link(p.memset(Mx[:, :, :, :, :].rearrange("p b s c j -> p (b s c j)"), 0.0))
            link(p.memset(kbd[:, :, :, :].rearrange("p b s k -> p (b s k)"), 0.0))
            link(p.memset(s16, 0.0))
            link(p.memset(vst[:, :, :, :].rearrange("p b c j -> p (b c j)"), 0.0))
            p.memset(vhead[:, :, :, :, HD].rearrange("p b c h -> p (b c) h"), 1.0).then_inc(presets, 1)
            p.memset(kw[:, :, :, :].rearrange("p r g k -> p (r g k)").bitcast(F32), 0.0).then_inc(presets, 1)
            if LAST == 1:
                return
            pool.wait_ge(par_in[1], 16)
            norm(1, "b_bp")
            if LAST == 2:
                return
            norm(2, None)
            if LAST == 3:
                return
            norm(3, None)
            link(p.memset(vhead[:, :, 0:NC, :, HD], 0.0))
            for b in range(B):
                t = tiles[("v", 3, b)]
                pool.wait_ge(t.drained, t.nth)
                p.tensor_copy(vhead[:, b, 0:NC, :, 0:HD], vtok[:, b].rearrange("p c (h d) -> p c h d", h=H)).then_inc(vpad_ready, 1)
            for b in range(B):
                pool.wait_ge(rms_ready, b + 1)
                p.tensor_tensor(f16h[5][:, b], f16h[2][:, b], neghalf[:, 0:NC * H], ALU.pow).then_inc(rms_pow, 1)
            if LAST == 4:
                return
            p.memset(vhead[:, :, 0:NC, :, HD], 1.0).then_inc(ones_ready, 1)
            pool.wait_ge(par_in[6], 16)
            norm(4, "e_bo")
            if LAST == 5:
                return
            norm(5, "f_b2")

        @block.sync
        def _(sp):
            def load_chunk(sp, n):
                a0 = P32[CHUNKS[n][0][0]][0]
                a1 = P32[CHUNKS[n][-1][0]][1]
                at = sum(w for ch in CHUNKS[:n] for _, w in ch)
                sp.dma_start(params[:, a0:a1], par[:, at:at + a1 - a0]).then_inc(par_in[n], 16)

            for b in range(B):
                sp.dma_start(X[:, b], x[b].rearrange("(c p) d -> p c d", p=128)).then_inc(x_in[b], 16)
                if b == 0:
                    load_chunk(sp, 0)
            sp.dma_start(halves[:, :], half).then_inc(half_in, 16)
            load_chunk(sp, 1)
            sp.dma_start(ctxk[:, :, :], ctx_kd.rearrange("b k d -> k b d")).then_inc(ctx_in, 16)
            sp.dma_start(lens_i[:, :], lens.unsqueeze(0).to_broadcast([128, B])).then_inc(small_in, 16)
            sp.dma_start(mask_u[:, :, :], maskb.unsqueeze(0).to_broadcast([128, B, KC])).then_inc(small_in, 16)
            for n in range(2, len(CHUNKS) - 1):
                load_chunk(sp, n)
            if LAST > 3:
                for b in range(B):
                    t = tiles[("y", 2, b)]
                    sp.wait_ge(t.filled, t.nth)
                load_chunk(sp, len(CHUNKS) - 1)
            takes = []
            for tag in ("d", "e"):
                if LAST <= {"d": 3, "e": 4}[tag]:
                    continue
                for j in range(B * SL):
                    s, b = j // B, j % B
                    t = tiles[("stk", tag, b, s)]
                    sp.wait_ge(t.drained, t.nth)
                    if len(takes) >= KR:
                        u = takes[-KR]
                        sp.wait_ge(u.filled, u.nth)
                    elif j == 0:
                        sp.wait_ge(presets, 2)
                    for g in range(G):
                        r = slice(32 * g, 32 * g + 32)
                        sp.dma_start(kw[r, j % KR, g], kst[r, b, s]).then_inc(kw_in[j % KR], 16)
                    takes.append(tiles[("of", s, b, G - 1) if tag == "d" else ("sc", tag, s, b, NC - 1, 1)])
            for b in range(B):
                residual_there(sp, LAST, b)
                sp.dma_start(out[b].rearrange("(c p) d -> p c d", p=128), X[:, b]).then_inc(out_done, 16)
            sp.wait_ge(half_in, 16)
            sp.wait_ge(ctx_in, 16)
            sp.wait_ge(small_in, 32)
            for n in range(len(CHUNKS) - (LAST <= 3)):
                sp.wait_ge(par_in[n], 16)
            sp.wait_ge(out_done, 16 * B)


def constants():
    f = np.float32
    p = np.arange(128)
    c = {"ident": np.eye(128, dtype=f)}
    row = p % 32
    col = lambda a: a.astype(f).reshape(128, -1)
    c["kconst"] = col(np.where(row == 0, -1.0, 0.0))
    c["kmask"] = col(np.where(row == 1, -BIG, 0.0))
    c["qconst"] = col(np.where(row == 1, BIG, 0.0))
    c["pos"] = col(p)
    c["posrow"] = np.broadcast_to(np.arange(KC, dtype=f), (128, KC))
    c["c_reset"] = np.broadcast_to((np.arange(NC * NE) % NE != 0).astype(f), (128, NC * NE))
    angle = np.repeat((1.0 / 10000.0 ** np.linspace(0.0, 1.0, HD // 2)).astype(f), 2)
    turn = (np.arange(S, dtype=f)[None, :] * angle[:, None]).astype(np.float64)
    gamma = 1.0 - 2.0 ** (-5.0 - np.arange(H))
    t = np.arange(S)
    up = gamma[:, None] ** (t % 128)[None, :]
    sign = np.where(np.arange(HD) % 2 == 0, -1.0, 1.0)[:, None]
    cos, sin = np.cos(turn), np.sin(turn) * sign
    full = lambda a, d: (a[None, :, :] * d[:, None, :]).reshape(128, S).astype(f)
    c["d_cosq"], c["d_sinq"] = full(cos, up), full(sin, up)
    down = D ** -0.5 / up
    c["d_cosk"], c["d_sink"] = full(cos, down), full(sin, down)
    c["d_tri"] = (p[:, None] <= p[None, :]).astype(f)
    head = p // HD
    c["d_gm"] = ((head[:, None] == head[None, :]) * (gamma[head] ** 128)[:, None]).astype(f)
    norm = 1.0 / np.sqrt(np.cumsum(gamma[:, None] ** t[None, :], axis=1))
    order = np.array([4 * g + s for s in range(SL) for g in range(G)])
    tn = norm[order].reshape(H, NC, 128).transpose(2, 1, 0)
    td = tn * (gamma[order][None, None, :] ** (128.0 * np.arange(NC))[None, :, None])
    c["d_tn"], c["d_td"] = col(tn), col(td)
    ones = np.zeros((128, NC, VW))
    ones[:, :, HD:H * (HD + 1):HD + 1] = (gamma[None, :] ** (-128.0 * np.arange(NC))[:, None])[None]
    c["d_one"] = col(ones)
    half = {"ident16": np.eye(128)}
    for name, rows in (("q_hi", (8, 16)), ("q_lo", (24,)), ("k_hi", (8, 24)), ("k_lo", (16,))):
        m = np.zeros((128, SL, 128))
        for g in range(G):
            for s in range(SL):
                for d in range(HD):
                    for r in rows:
                        m[32 * g + 8 * s + d, s, 32 * g + r + d] = 1.0
        half[name] = m.reshape(128, -1)
    e = np.zeros((128, NE, 128))
    for i in range(NE):
        e[i, i] = 1.0
        e[32 + i, i] = 1.0
    half["sel_e"] = e.reshape(128, -1)
    return c, np.concatenate([half[n].astype(np.float16) for n, _ in HALVES], axis=1)


def kernel(x, ctx_1024, _lenS2, mask_BxS2_bk0, **w):
    import concourse.bacc as bacc
    from concourse.bass_utils import run_bass_kernel_spmd

    arr = {k: np.asarray(v) for k, v in w.items()}
    ctx = np.ascontiguousarray(ctx_1024)
    c, half = constants()
    bc = lambda a: np.broadcast_to(a[None, :], (128, a.shape[0]))
    c["ctxT"] = ctx.transpose(2, 0, 1).reshape(128, B * KC)
    wqkv = arr["L0_attn_w_qkv"]
    c["a_wq"], c["a_wk"], c["a_wv"] = (wqkv[n * 128:(n + 1) * 128].T for n in range(3))
    c["a_wp"], c["a_bp"] = arr["L0_attn_w_proj"].T, bc(arr["L0_attn_b_proj"])
    kvw, kvb = arr["L0_xattn_kv_w"], arr["L0_xattn_kv_b"]
    c["b_wq"], c["b_wk"], c["b_wv"] = arr["L0_xattn_q_w"].T, kvw[0:128].T, kvw[128:256].T
    c["b_wp"], c["b_bp"], c["b_vb"] = arr["L0_xattn_proj_w"].T, bc(arr["L0_xattn_proj_b"]), bc(kvb[128:256])
    c["b_qb"], c["b_kb"] = arr["L0_xattn_q_b"].reshape(128, 1), kvb[0:128].reshape(128, 1)
    c["c_wg"] = arr["L0_ffn_Wg"]
    c["c_b1"] = arr["L0_ffn_b1"].reshape(2 * NE, 128).T
    c["c_b2"] = np.concatenate([arr["L0_ffn_b2"], np.zeros((128 - NE, 128), np.float32)])
    c["c_w1"] = arr["L0_ffn_W1"].transpose(1, 0, 2).reshape(128, NE * FE)
    c["c_w2"] = arr["L0_ffn_W2"].reshape(2 * NE, 128, 128).transpose(1, 0, 2).reshape(128, NE * FE)
    swap = np.arange(128) ^ 1
    c["d_wq"], c["d_wk"] = arr["L1_attn_Wq"], arr["L1_attn_Wk"]
    c["d_wqs"], c["d_wks"] = c["d_wq"][:, swap], c["d_wk"][:, swap]
    c["d_wv"], c["d_wg"] = arr["L1_attn_Wv"], arr["L1_attn_Wg"]
    for n in "qkvo":
        c["e_w" + n] = arr["L1_xattn_w" + n].T
    c["e_bo"], c["f_b2"] = bc(arr["L1_xattn_bo"]), bc(arr["L1_ffn_b2"])
    for n, a in (("f_b1", "b1"), ("f_th", "quantum_phases"), ("f_wr", "quantum_weights_real"), ("f_wi", "quantum_weights_imag")):
        c[n] = arr["L1_ffn_" + a].reshape(NJ, 128).T
    c["f_w1"] = arr["L1_ffn_W1"]
    c["f_w2"] = arr["L1_ffn_W2"].reshape(NJ, 128, 128).transpose(1, 0, 2).reshape(128, NJ * 128)
    par = np.concatenate([c[n] for ch in CHUNKS for n, _ in ch], axis=1)
    assert par.shape == (128, WIDTH) and half.shape == (128, HWIDTH)

    nc = bacc.Bacc("TRN2", target_bir_lowering=False, num_devices=1)
    arrays = {"x_dram": np.ascontiguousarray(x), "ctx_dram": ctx, "len_dram": np.ascontiguousarray(_lenS2),
              "mask_dram": np.ascontiguousarray(mask_BxS2_bk0), "par_dram": np.ascontiguousarray(par),
              "half_dram": half}
    aps = [nc.dram_tensor(n, a.shape, mybir.dt.from_np(a.dtype), kind="ExternalInput").ap() for n, a in arrays.items()]
    out = nc.dram_tensor("out_dram", (B, S, D), F32, kind="ExternalOutput").ap()
    decoder(nc, *aps, out)
    r = run_bass_kernel_spmd(nc, [arrays], core_ids=[0])
    return r.results[0]["out_dram"]
```

```python
import itertools
from contextlib import ExitStack

import numpy as np

import concourse.bass as bass
from concourse import mybir

F32 = mybir.dt.float32
F16 = mybir.dt.float16
U8 = mybir.dt.uint8
I32 = mybir.dt.int32
ALU = mybir.AluOpType
ACT = mybir.ActivationFunctionType
AX = mybir.AxisListType

B, S, D = 2, 512, 128
NC = S // 128
H, HD, G, SL = 16, 8, 4, 4
KC = 77
NE, FE = 8, 256
FF = 512
NJ = FF // 128
SCALE = HD ** -0.5
BIG = 60000.0
LN_EPS = 1e-5
RMS_EPS = 1e-6
ROUND = 1.5 * 2.0 ** 23
TWO_PI = 2.0 * np.pi
PI_A = 6.28125
PI_B = float(np.float32(np.round((TWO_PI - PI_A) * 2 ** 21) / 2 ** 21))
PI_C = float(np.float32(TWO_PI - PI_A - PI_B))
TURN = float(np.nextafter(np.float32(TWO_PI), np.float32(0)))
PK = S + KC
VW = H * (HD + 1) + 32 - (HD + 1)
KR = 4

CHUNKS = [
    [("ident", 128), ("a_wq", 128), ("a_wk", 128), ("a_wv", 128), ("a_wp", 128), ("a_bp", 128)],
    [("b_wq", 128), ("b_wk", 128), ("b_wv", 128), ("b_wp", 128), ("b_bp", 128), ("b_vb", 128),
     ("b_qb", 1), ("b_kb", 1), ("kconst", 1), ("kmask", 1), ("qconst", 1), ("pos", 1),
     ("posrow", KC), ("ctxT", B * KC)],
    [("c_wg", NE), ("c_b1", 2 * NE), ("c_reset", NC * NE), ("c_b2", 128), ("c_w1", NE * FE)],
    [("c_w2", NE * FE)],
    [("d_wq", 128), ("d_wqs", 128), ("d_wk", 128), ("d_wks", 128), ("d_wv", 128), ("d_wg", 128),
     ("d_cosq", S), ("d_sinq", S), ("d_cosk", S), ("d_sink", S)],
    [("d_tri", 128), ("d_gm", 128), ("d_tn", NC * H), ("d_td", NC * H), ("d_one", NC * VW)],
    [("e_wq", 128), ("e_wk", 128), ("e_wv", 128), ("e_wo", 128), ("e_bo", 128),
     ("f_b2", 128), ("f_b1", NJ), ("f_th", NJ), ("f_wr", NJ), ("f_wi", NJ),
     ("f_w1", FF), ("f_w2", FF)],
]
WIDTH = sum(n for ch in CHUNKS for _, n in ch)
LATE = sum(n for _, n in CHUNKS[-1])
assert LATE <= NE * FE
HALVES = [("ident16", 128), ("q_hi", SL * 128), ("q_lo", SL * 128), ("k_hi", SL * 128), ("k_lo", SL * 128),
          ("sel_e", NE * 128)]
HWIDTH = sum(n for _, n in HALVES)


def offsets(pairs):
    at, out = 0, {}
    for name, n in pairs:
        out[name] = (at, at + n)
        at += n
    return out


def decoder(nc, x, ctx_kd, lens, maskb, par, half, out):
    P32 = offsets([p for ch in CHUNKS for p in ch])
    P16 = offsets(HALVES)
    stack = ExitStack()
    with stack:
        def sb(name, shape, dt=F32):
            return stack.enter_context(nc.sbuf_tensor(name, shape, dt))

        def sem(name):
            return stack.enter_context(nc.semaphore(name))

        params = sb("params", [128, WIDTH - LATE])
        halves = sb("halves", [128, HWIDTH], F16)

        for name, _ in CHUNKS[-1]:
            P32[name] = tuple(a - (WIDTH - LATE) + P32["c_w1"][0] for a in P32[name])

        def par_of(name):
            return params[:, P32[name][0]:P32[name][1]]

        def half_of(name):
            return halves[:, P16[name][0]:P16[name][1]]

        ident = par_of("ident")
        ident16 = half_of("ident16")

        X = sb("X", [128, B, NC, 128])
        R = sb("R", [128, B, NC, 128])
        ctxk = sb("ctxk", [KC, B, 128])
        lens_i = sb("lens_i", [128, B], I32)
        mask_u = sb("mask_u", [128, B, KC], U8)
        bn = sb("bn", [128, B, NC, 6])
        mv = sb("mv", [128, B, NC, 2])
        veps = sb("veps", [128, B, NC])
        rstd = sb("rstd", [128, B, NC])
        neghalf = sb("neghalf", [128, NC])
        xn = sb("xn", [128, B, NC, 128])
        xnT = sb("xnT", [128, B, S])
        qT = sb("qT", [128, B, S])
        kT = sb("kT", [128, B, S])
        vtok = sb("vtok", [128, B, NC, 128])
        negmax = sb("negmax", [128, B, NC])
        rowsum = sb("rowsum", [128, B, NC])
        rinv = sb("rinv", [128, B, NC])
        big = sb("big", [128, 16, 512])
        PT = sb("PT", [128, 8, 512])
        Osb = sb("Osb", [128, B, NC, 128])
        hi_flat = sb("hi", [128, B * 2 * PK], F16)
        hi = hi_flat[:, :].rearrange("p (b w k) -> p b w k", b=B, w=2)
        lo = sb("lo", [128, B, 2, PK], F16)
        qst = sb("qst", [128, B, SL, S], F16)
        kst = sb("kst", [128, B, SL, S], F16)
        kbd = sb("kbd", [128, B, SL, G * KC], F16)
        kadd = sb("kadd", [128, B, KC], F32)
        kw = sb("kw", [128, KR, G, S], F16)
        vst = sb("vst", [128, B, NC + 1, VW])
        vhead = vst[:, :, :, 0:H * (HD + 1)].rearrange("p b c (h j) -> p b c h j", h=H)
        Mx = sb("Mx", [128, B, SL, NC, 128], F16)
        Mp = sb("Mp", [128, 2, NC * G])
        Mn = sb("Mn", [128, 2, NC * G])
        oT = PT[:, :, :].rearrange("p (b s) q -> p b s q", b=B)
        rden = sb("rden", [128, B, NC, SL, G])
        on, onT = Osb, qT
        lens_f = sb("lens_f", [128, B])
        maxlen = sb("maxlen", [128, 1])
        kpast = sb("kpast", [128, B, KC])
        posm = sb("posm", [128, B, KC])
        vkeep = sb("vkeep", [128, B])
        small = [sb(f"small{n}", [128, B, NC, NE]) for n in range(10)]
        thin = [sb(f"thin{n}", [128, B, NC]) for n in range(3)]
        s16 = kst[:, :, 0]
        s32 = kT[0:NE]
        rot = PT[:, :, :].rearrange("p (b w) q -> p b w q", b=B)
        ktok = Osb
        first = params[:, P32["a_wq"][0]:P32["b_vb"][1]]
        second = par_of("c_w2")
        th = [w[:, 0:512].rearrange("p (c d) -> p c d", c=NC) for w in (first, second)]
        state = [w[:, 512:896].rearrange("p (c d) -> p c d", c=3) for w in (first, second)]
        stmp = [w[:, 896:1024] for w in (first, second)]
        cross = onT[:, :, :].rearrange("p b (c d) -> p b c d", c=NC)
        f16h = [sb(f"fh{n}", [128, B, NC * H]) for n in range(6)]
        Aoff = [sb(f"Aoff{n}", [128, 768])[:, :] for n in range(3)]
        Aoff.append(second[:, 1024:1792])
        tv = [sb(f"tv{n}", [128, NJ]) for n in range(10)]
        n0, fold, absr, cosn, phs, amp, a1, a2, sin_v, cos_v = tv

        pair = [stack.enter_context(nc.psum_tensor(f"pair{n}", [128, 2, 512], F32)) for n in range(2)]
        one = [stack.enter_context(nc.psum_tensor(f"one{n}", [128, 512], F32)) for n in range(4)]
        filled = [sem(f"filled{n}") for n in range(6)]
        drained = [sem(f"drained{n}") for n in range(6)]

        class Tile:
            pass

        tiles, uses, turn = {}, [0] * 6, {}

        def claim(pe, key, ring):
            n = turn.get(ring, 0)
            turn[ring] = n + 1
            t = Tile()
            u = ring[n % len(ring)]
            t.wide = pair[u] if u < 2 else None
            t.ap = pair[u][:, 0] if u < 2 else one[u - 2][:, :]
            t.filled, t.drained = filled[u], drained[u]
            if uses[u]:
                pe.wait_ge(t.drained, uses[u])
            uses[u] += 1
            t.nth = uses[u]
            assert key not in tiles, key
            tiles[key] = t
            return t

        x_in = [sem(f"x_in{b}") for b in range(B)]
        par_in = [sem(f"par_in{n}") for n in range(len(CHUNKS))]
        half_in = sem("half_in")
        ctx_in = sem("ctx_in")
        small_in = sem("small_in")
        presets = sem("presets")
        stats_ready = sem("stats_ready")
        rstd_ready = sem("rstd_ready")
        xn_ready = sem("xn_ready")
        res_ready = sem("res_ready")
        bias_ready = sem("bias_ready")
        max_ready = sem("max_ready")
        rinv_ready = sem("rinv_ready")
        out_done = sem("out_done")
        dve_step = sem("dve_step")
        pool_step = sem("pool_step")
        hi_ready = sem("hi_ready")
        lo_ready = sem("lo_ready")
        kadd_ready = sem("kadd_ready")
        mx_ready = sem("mx_ready")
        p_used = sem("p_used")
        vpast_ready = sem("vpast_ready")
        diff_ready = sem("diff_ready")
        e_ready = sem("e_ready")
        score_ready = sem("score_ready")
        g_ready = sem("g_ready")
        g_used = sem("g_used")
        rot_ready = sem("rot_ready")
        th_ready = sem("th_ready")
        vpad_ready = sem("vpad_ready")
        absd_ready = sem("absd_ready")
        off_used = sem("off_used")
        state_ready = sem("state_ready")
        rms_ready = sem("rms_ready")
        num_ready = sem("num_ready")
        gated_ready = sem("gated_ready")
        root_ready = sem("root_ready")
        fold_ready = sem("fold_ready")
        phase_ready = sem("phase_ready")
        sinv_ready = sem("sinv_ready")
        wrap_ready = sem("wrap_ready")
        hi16_ready = sem("hi16_ready")
        kw_in = [sem(f"kw_in{n}") for n in range(KR)]
        ones_ready = sem("ones_ready")
        sine_ready = sem("sine_ready")
        mix_ready = sem("mix_ready")
        act_ready = sem("act_ready")

        block = stack.enter_context(nc.Block())

        quads_used = []

        def residual_there(eng, l, b):
            if l == 0:
                eng.wait_ge(x_in[b], 16)
            elif l == 4:
                eng.wait_ge(res_ready, b + 1)
            else:
                t = tiles[("y", l - 1, b)]
                eng.wait_ge(t.drained, t.nth)

        def window(a, n):
            return a[:, (HD + 1) * n:(HD + 1) * n + 32]

        def used_diagonals(eng, j):
            t = tiles[("nt", j % SL, j // SL)]
            eng.wait_ge(t.filled, t.nth)

        UNITS = [(l, b) for l in range(5) for b in range(B)]
        ALL = (2, 3, 4, 5, 0, 1)
        MOE_RING = [(0, 1, 2, 3, 5), (0, 1, 2, 3, 4)]
        RINGS = {0: ALL, 1: (2, 3), 3: (2, 3, 4), 4: (2, 3, 4)}
        PACE = {(0, 0): 1, (0, 1): 1, (1, 0): 1.5, (1, 1): 2, (2, 0): 1, (2, 1): 1, (3, 0): 1.1, (3, 1): 2.2,
                (4, 0): 1, (4, 1): 1}
        LEAD = {(1, 0): 4}
        LAST_IDLE = 9
        FF_PAUSE = 15
        CONTEXT_AT = (2, 1)

        def idle(l, b):
            return {0: 0, 1: 4, 2: 1, 3: 6, 4: 3}[l] if b < B - 1 else 0

        def key_tiles(tag):
            return [(NC, KC, True)] if tag == "b" else [(n, 128, False) for n in range(NC)] + [(NC, KC, True)]

        def groups_of(tag):
            return [-1] if tag == "b" else [0, 1, 2, 3, -1]

        def max_list(tag, j):
            return [(c, g) for c in range(NC) for g in groups_of(tag)]

        LEADING = {"b": 2, "e": 1}
        MAX_PACE = {"b": 2, "e": 2.5}

        def ahead(tag, j, n):
            every = [(i, c, g) for i in range(LEADING[tag], B * SL) for c, g in max_list(tag, i)]
            step = 2 * len(key_tiles(tag)) * j + n
            return every[int(MAX_PACE[tag] * step):int(MAX_PACE[tag] * (step + 1))]

        def shift_step(tag):
            return 0 if tag == "b" else 8

        MIX_AT = (2, 4, 6, 7)

        def wrapped(b, j):
            return (xn[:, b].rearrange("p c d -> p (c d)"), onT[:, b], on[:, b].rearrange("p c d -> p (c d)"),
                    vtok[:, b].rearrange("p c d -> p (c d)"))[j]

        def weave(context, begin, bulk, end):
            for _ in zip(begin(0, 0), begin(0, 1)):
                pass
            for n, (l, b) in enumerate(UNITS):
                side = [context()] if n == 0 else []
                if n:
                    side.append(end(*UNITS[n - 1]))
                if n == len(UNITS) - 1:
                    side.append(begin(5, 0))
                elif n >= 1:
                    side.append(begin(*UNITS[n + 1]))
                side = itertools.chain(*side)
                for _ in range(LEAD.get((l, b), 0)):
                    next(side, None)
                for k, _ in enumerate(bulk(l, b)):
                    for _ in range(int((k + 1) * PACE[l, b]) - int(k * PACE[l, b])):
                        next(side, None)
                if n < len(UNITS) - 1:
                    for _ in side:
                        pass
            for _ in itertools.chain(end(*UNITS[-1]), begin(5, 1)):
                next(side, None)
            for _ in side:
                pass

        def head_bulk(tag, l, b, start, half):
            if b == 0:
                start()
            keys = key_tiles(tag)
            for s in range(SL):
                for n in range(2 * len(keys)):
                    half(b * SL + s, n, keys)
                    yield

        @block.tensor
        def _(pe):
            ring = [ALL]

            def norm_T(l, b):
                pe.wait_ge(xn_ready, l * B + b + 1)
                if l == 0 and b == 0:
                    pe.wait_ge(par_in[0], 16)
                t = claim(pe, ("xT", l, b), ring[0])
                for c in range(NC):
                    mm = pe.transpose(t.ap[:, c * 128:(c + 1) * 128], xn[:, b, c, :], ident)
                mm.then_inc(t.filled, 1)

            def feature_major(key, w, b, n=S, rhs=None):
                t = claim(pe, key, ring[0])
                pe.matmul(t.ap[:, 0:n], w, xnT[:, b] if rhs is None else rhs, start=True, stop=True).then_inc(t.filled, 1)

            def token_major(key, lhs, w, wn=128):
                t = claim(pe, key, ring[0])
                for c in range(NC):
                    mm = pe.matmul(t.ap[:, c * wn:(c + 1) * wn], lhs[:, c * 128:(c + 1) * 128], w, start=True, stop=True)
                mm.then_inc(t.filled, 1)

            def ready(key):
                t = tiles[key]
                pe.wait_ge(t.drained, t.nth)

            def expand(o, which, b, s, src):
                names = ("k_hi", "k_lo") if which else ("q_hi", "q_lo")
                pe.matmul(o, half_of(names[0])[:, s * 128:(s + 1) * 128], hi[:, b, which, src], start=True, stop=False)
                return pe.matmul(o, half_of(names[1])[:, s * 128:(s + 1) * 128], lo[:, b, which, src], start=False, stop=True)

            def context_stack(tag, b):
                if tag == "b":
                    ready(("kT", 1, b))
                else:
                    pe.wait_ge(lo_ready, b + 1)
                t = claim(pe, ("kc", tag, b), ring[0])
                for s in range(SL):
                    mm = expand(t.ap[:, s * KC:(s + 1) * KC], 1, b, s, slice(S, PK))
                mm.then_inc(t.filled, 1)

            def stacks(tag, which, b, slots=range(SL)):
                if tag == "d":
                    pe.wait_ge(lo_ready, B + 2 * b + which + 1)
                else:
                    ready((("qT", "kT")[which], {"b": 1, "e": 4}[tag], b))
                for s in slots:
                    t = claim(pe, ("st" + "qk"[which], tag, b, s), ring[0])
                    expand(t.ap, which, b, s, slice(0, S)).then_inc(t.filled, 1)

            def widened(j, tag):
                uses_before = (B * SL if tag == "e" else 0) + j
                pe.wait_ge(kw_in[j % KR], 64 * (uses_before // KR + 1))

            MAXR = {"b": (2, 3), "e": (2, 3, 4)}

            def shift_T(tag, j):
                b, s = j // SL, j % SL
                if tag == "b":
                    ready(("mx", tag, j, NC - 1, -1))
                else:
                    pe.wait_ge(mx_ready, j + 1)
                t = claim(pe, ("mT", tag, j), MAXR[tag])
                to = t.ap.bitcast(F16)
                for c in range(NC):
                    mm = pe.transpose(to[:, c * 128:(c + 1) * 128], Mx[:, b, s, c], ident16)
                mm.then_inc(t.filled, 1)

            def max_tile(tag, j, c, g):
                b, s = j // SL, j % SL
                if c == 0 and g == groups_of(tag)[0]:
                    if s == 0:
                        ready(("kc", tag, b))
                    ready(("stq", tag, b, s))
                    if tag == "e":
                        widened(j, tag)
                t = claim(pe, ("mx", tag, j, c, g), MAXR[tag])
                q = qst[:, b, s, c * 128:(c + 1) * 128]
                if g < 0:
                    pe.matmul(t.ap[:, 0:G * KC], q, kbd[:, b, s], start=True, stop=True).then_inc(t.filled, 1)
                else:
                    pe.matmul(t.ap, q, kw[:, j % KR, g], start=True, stop=True).then_inc(t.filled, 1)

            def score_tile(tag, j, k, nk, past, gp):
                b, s = j // SL, j % SL
                t = claim(pe, ("sc", tag, j, k, gp), (0, 1))
                for i in range(2):
                    g = 2 * gp + i
                    keys = kbd[:, b, s, g * KC:(g + 1) * KC] if past else kw[:, j % KR, g, k * 128:(k + 1) * 128]
                    mm = pe.matmul(t.wide[0:nk, i], keys, qst[:, b, s], start=True, stop=True)
                mm.then_inc(t.filled, 1)

            p_taken, early = [0], [0]

            def values(tag, j, k, nk, first, last):
                b, s = j // SL, j % SL
                if first:
                    claim(pe, ("ov", tag, j), (4, 5) if tag == "b" else (5,))
                    if s == 0:
                        ready(("v", {"b": 1, "e": 4}[tag], b))
                        if tag == "e":
                            pe.wait_ge(vpast_ready, b + 1)
                            pe.wait_ge(ones_ready, b + 1)
                t = tiles[("ov", tag, j)]
                p_taken[0] += 2
                ready(("sc", tag, j, k, 1))
                for g in range(G):
                    buf = (p_taken[0] - 2 + g // 2) % 8
                    mm = pe.matmul(t.ap[32 * g:32 * g + 32], window(vst[0:nk, b, k], 4 * g + s),
                                   big[0:nk, 2 * buf + g % 2], start=first, stop=last)
                if last:
                    mm.then_inc(t.filled, 1)
                    quads_used.append((t.filled, t.nth))
                else:
                    mm.then_inc(p_used, 1)
                    early[0] += 1
                    quads_used.append((p_used, early[0]))

            def heads(tag, l, b):
                def start():
                    for j in range(LEADING[tag] if tag == "b" else 0):
                        for m in max_list(tag, j):
                            max_tile(tag, j, *m)
                    shift_T(tag, 0)

                def half(j, n, keys):
                    k, gp = n // 2, n % 2
                    if n == 0:
                        ready(("mT", tag, j))
                    score_tile(tag, j, *keys[k], gp)
                    maxima = ahead(tag, j, n)
                    late = maxima[-1:] if gp == 1 and tag == "e" else []
                    for m in maxima[:len(maxima) - len(late)]:
                        max_tile(tag, *m)
                    if n == shift_step(tag) and j + 1 < B * SL:
                        shift_T(tag, j + 1)
                    if gp == 1 and k >= 1:
                        values(tag, j, *keys[k - 1][:2], k == 1, False)
                    if n == 1 and j >= 1:
                        values(tag, j - 1, *keys[-1][:2], len(keys) == 1, True)
                    for m in late:
                        max_tile(tag, *m)

                yield from head_bulk(tag, l, b, start, half)
                if b == B - 1:
                    values(tag, B * SL - 1, *key_tiles(tag)[-1][:2], tag == "b", True)

            def context():
                for _ in range(3):
                    yield
                pe.wait_ge(par_in[1], 16)
                pe.wait_ge(half_in, 16)
                for b in range(B):
                    cT = par_of("ctxT")[:, b * KC:(b + 1) * KC]
                    feature_major(("kT", 1, b), par_of("b_wk"), b, KC, cT)
                    t = claim(pe, ("v", 1, b), ring[0])
                    pe.matmul(t.ap[0:KC, 0:128], cT, par_of("b_wv"), start=True, stop=True).then_inc(t.filled, 1)
                yield
                for b in range(B):
                    context_stack("b", b)
                yield

            def begin(l, b):
                if (l, b) == (5, 0):
                    for _ in range(LAST_IDLE):
                        yield
                yield
                yield
                if l == 4:
                    if b == 0:
                        pe.wait_ge(par_in[6], 16)
                yield
                if (l, b) == CONTEXT_AT:
                    for i in range(B):
                        context_stack("e", i)
                yield
                norm_T(l, b)
                yield
                ready(("xT", l, b))
                if l == 0:
                    feature_major(("qT", 0, b), par_of("a_wq"), b)
                    feature_major(("kT", 0, b), par_of("a_wk"), b)
                    token_major(("v", 0, b), xnT[:, b], par_of("a_wv"))
                    yield
                if l == 1:
                    feature_major(("qT", 1, b), par_of("b_wq"), b)
                    yield
                    stacks("b", 0, b, (0, 1))
                    yield
                    stacks("b", 0, b, (2, 3))
                    yield
                if l == 2:
                    if b == 0:
                        pe.wait_ge(par_in[2], 16)
                    token_major(("lg", b), xnT[:, b], par_of("c_wg"), NE)
                    yield
                    yield
                    pe.wait_ge(score_ready, b + 1)
                    t = claim(pe, ("sT", b), ring[0])
                    for c in range(NC):
                        mm = pe.transpose(t.ap[0:NE, c * 128:(c + 1) * 128], small[9][:, b, c], ident)
                    mm.then_inc(t.filled, 1)
                    yield
                if l == 3:
                    if b == 0:
                        pe.wait_ge(par_in[4], 16)
                        pe.wait_ge(par_in[5], 16)
                    for n, w in enumerate(("d_wq", "d_wqs", "d_wk", "d_wks")):
                        feature_major(("r", b, n), par_of(w), b)
                        if n % 2:
                            yield
                    token_major(("v", 3, b), xnT[:, b], par_of("d_wv"))
                    token_major(("gate", b), xnT[:, b], par_of("d_wg"))
                    yield
                    pe.wait_ge(rot_ready, 2 * b + 2)
                    token_major(("ktok", b), rot[:, b, 1], ident)
                    stacks("d", 1, b, (0, 1))
                    yield
                    stacks("d", 1, b, (2, 3))
                    yield
                    stacks("d", 0, b, (0, 1))
                    yield
                    stacks("d", 0, b, (2, 3))
                    yield
                    ready(("ktok", b))
                    ready(("v", 3, b))
                    for c in range(NC - 1):
                        t = claim(pe, ("kv", b, c), ring[0])
                        pe.matmul(t.ap[:, 0:128], ktok[:, b, c], vtok[:, b, c], start=True, stop=True).then_inc(t.filled, 1)
                    yield
                    yield
                    t = claim(pe, ("cr", b), ring[0])
                    for c in range(1, NC):
                        if c == 1:
                            ready(("kv", b, 0))
                        else:
                            pe.wait_ge(state_ready, b * (NC - 2) + c - 1)
                        mm = pe.matmul(t.ap[:, c * 128:(c + 1) * 128], rot[:, b, 0, c * 128:(c + 1) * 128],
                                       state[b][:, c - 1], start=True, stop=True)
                    mm.then_inc(t.filled, 1)
                    yield
                if l == 4:
                    feature_major(("kT", 4, b), par_of("e_wk"), b)
                    feature_major(("qT", 4, b), par_of("e_wq"), b)
                    yield
                    stacks("e", 1, b, (0, 1))
                    yield
                    stacks("e", 1, b, (2, 3))
                    yield
                    stacks("e", 0, b, (0, 1))
                    yield
                    stacks("e", 0, b, (2, 3))
                    yield
                    token_major(("v", 4, b), xnT[:, b], par_of("e_wv"))
                    yield
                    if b == 0:
                        for n, m in enumerate(max_list("e", 0)):
                            max_tile("e", 0, *m)
                            if n % 2:
                                yield
                if l == 5:
                    for j in range(NJ):
                        feature_major(("f1", b, j), par_of("f_w1")[:, j * 128:(j + 1) * 128], b)
                        yield
                    if b == 0:
                        for _ in range(FF_PAUSE + 12):
                            yield
                    else:
                        yield
                    t = claim(pe, ("y", 5, b), ring[0])
                    for j in range(NJ):
                        pe.wait_ge(act_ready, b * NJ + j + 1)
                        for c in range(NC):
                            mm = pe.matmul(t.ap[:, c * 128:(c + 1) * 128], PT[:, NJ * b + j, c * 128:(c + 1) * 128],
                                           par_of("f_w2")[:, j * 128:(j + 1) * 128], start=(j == 0 and c == 0),
                                           stop=(j == NJ - 1), skip_group_check=True)
                    mm.then_inc(t.filled, 1)
                    yield
                    yield
                    yield

            def self_attention(b):
                ready(("qT", 0, b))
                ready(("kT", 0, b))
                for c in range(NC):
                    t = claim(pe, ("s", b, c), ALL)
                    pe.matmul(t.ap, qT[:, b, c * 128:(c + 1) * 128], kT[:, b], start=True, stop=True).then_inc(t.filled, 1)
                    yield
                for c in range(NC):
                    t = claim(pe, ("pT", b, c), ALL)
                    ready(("s", b, c))
                    for k in range(NC):
                        mm = pe.transpose(t.ap[:, k * 128:(k + 1) * 128], big[:, b * NC + c, k * 128:(k + 1) * 128], ident)
                    mm.then_inc(t.filled, 1)
                    yield
                ready(("v", 0, b))
                t = claim(pe, ("o", 0, b), ALL)
                for c in range(NC):
                    ready(("pT", b, c))
                    for k in range(NC):
                        mm = pe.matmul(t.ap[:, c * 128:(c + 1) * 128], PT[:, b * NC + c, k * 128:(k + 1) * 128],
                                       vtok[:, b, k], start=(k == 0), stop=(k == NC - 1))
                mm.then_inc(t.filled, 1)
                yield

            g_taken = [0]

            def down(e, b):
                if e == 0:
                    claim(pe, ("y", 2, b), (4 + b,))
                y = tiles[("y", 2, b)]
                for hf in range(2):
                    if hf == 0:
                        pe.wait_ge(g_ready, g_taken[0] // 2 + 1)
                    else:
                        ready(("sb", e, b))
                    buf = g_taken[0] % 8
                    g_taken[0] += 1
                    for c in range(NC):
                        mm = pe.matmul(y.ap[:, c * 128:(c + 1) * 128], big[:, 8 + buf, c * 128:(c + 1) * 128],
                                       par_of("c_w2")[:, (2 * e + hf) * 128:(2 * e + hf + 1) * 128],
                                       start=(e == 0 and hf == 0 and c == 0), stop=False, skip_group_check=True)
                    mm.then_inc(g_used, 1)
                if e == NE - 1:
                    for c in range(NC):
                        mm = pe.matmul(y.ap[:, c * 128:(c + 1) * 128], s32[:, b, c * 128:(c + 1) * 128],
                                       par_of("c_b2")[0:NE, :], start=False, stop=(c == NC - 1), skip_group_check=True)
                    mm.then_inc(y.filled, 1)

            def experts(b):
                ready(("sT", b))
                if b == 0:
                    pe.wait_ge(par_in[3], 16)
                for e in range(NE):
                    t = claim(pe, ("sb", e, b), ring[0])
                    pe.matmul(t.ap, half_of("sel_e")[:, e * 128:(e + 1) * 128], s16[:, b], start=True,
                              stop=True).then_inc(t.filled, 1)
                    for hf in range(2):
                        t = claim(pe, ("h", e, b, hf), ring[0])
                        w = par_of("c_w1")[:, e * FE + hf * 128:e * FE + (hf + 1) * 128]
                        pe.matmul(t.ap, w, xnT[:, b], start=True, stop=True).then_inc(t.filled, 1)
                    yield
                    if e >= 1:
                        down(e - 1, b)
                    elif b >= 1:
                        down(NE - 1, b - 1)
                    yield
                if b == B - 1:
                    down(NE - 1, b)

            def ones_of(c):
                return par_of("d_one")[:, c * VW:(c + 1) * VW]

            def ret_scores(j, g):
                b, s = j // SL, j % SL
                keys = kw[:, j % KR, g]
                t = claim(pe, ("dg", j, g), (2, 3, 4))
                for c in range(NC):
                    w = slice(c * 128, (c + 1) * 128)
                    mm = pe.matmul(t.ap[:, w], keys[:, w], qst[:, b, s, w], start=True, stop=True)
                mm.then_inc(t.filled, 1)
                t = claim(pe, ("of", j, g), (0, 1))
                pe.matmul(t.wide[:, 0, 0:384], keys[:, 0:128], qst[:, b, s, 128:512], start=True, stop=True)
                pe.matmul(t.wide[:, 0, 384:512], keys[:, 256:384], qst[:, b, s, 384:512], start=True, stop=True)
                pe.matmul(t.wide[:, 1, 0:256], keys[:, 128:256], qst[:, b, s, 256:512], start=True,
                          stop=True).then_inc(t.filled, 1)

            def far_sums(j):
                b, s = j // SL, j % SL
                t = claim(pe, ("nt", s, b), (5,))
                for g in range(G):
                    ready(("of", j, g))
                    A = Aoff[g]
                    o = t.ap[32 * g:32 * g + 32]
                    wa = [window(ones_of(c), 4 * g + s) for c in range(3)]
                    pe.matmul(o[:, 128:512], wa[0], A[:, 0:384], start=True, stop=False, skip_group_check=True)
                    pe.matmul(o[:, 384:512], wa[2], A[:, 384:512], start=False, stop=False, skip_group_check=True)
                    pe.matmul(o[:, 256:512], wa[1], A[:, 512:768], start=False, stop=False,
                              skip_group_check=True).then_inc(off_used, 1)

            def near_sums(j, blocks):
                b, s = j // SL, j % SL
                t = tiles[("nt", s, b)]
                pe.wait_ge(absd_ready, 4 * j + 4)
                for c in blocks:
                    w = slice(c * 128, (c + 1) * 128)
                    for g in range(G):
                        pe.matmul(t.ap[32 * g:32 * g + 32, w], window(ones_of(c), 4 * g + s),
                                  big[:, 8 + (4 * j + g) % 8, w], start=False, stop=False, skip_group_check=True)
                    for g in range(G):
                        mm = pe.matmul(t.ap[32 * g:32 * g + 32, w], window(vst[:, b, c], 4 * g + s), big[:, (4 * j + g) % 8, w],
                                       start=False, stop=(c == NC - 1), skip_group_check=True)
                if blocks[-1] == NC - 1:
                    mm.then_inc(t.filled, 1)

            def retention(b):
                for s in range(SL):
                    ready(("stq", "d", b, s))
                pe.wait_ge(vpad_ready, b + 1)
                for n in range(H * b, H * b + H):
                    j, g = n // G, n % G
                    if g == 0:
                        widened(j, "d")
                    ret_scores(j, g)
                    if g == 0 and j:
                        far_sums(j - 1)
                    if g in (1, 2) and j:
                        near_sums(j - 1, ((0, 1), (2, 3))[g - 1])
                    yield
                if b == B - 1:
                    far_sums(B * SL - 1)
                    near_sums(B * SL - 1, (0, 1, 2, 3))

            def bulk(l, b):
                ring[0] = MOE_RING[b] if l == 2 else RINGS[l]
                yield from (self_attention(b) if l == 0 else heads("b", l, b) if l == 1 else experts(b) if l == 2
                            else retention(b) if l == 3 else heads("e", l, b))
                if (l, b) == UNITS[-1]:
                    ring[0] = ALL

            def end(l, b):
                for _ in range(idle(l, b)):
                    yield
                if l == 0:
                    ready(("o", 0, b))
                    token_major(("y", 0, b), Osb[:, b].rearrange("p c d -> p (c d)"), par_of("a_wp"))
                    yield
                if l in (1, 4):
                    tag = "b" if l == 1 else "e"
                    for c in range(NC):
                        t = claim(pe, ("on", tag, b, c), ring[0])
                        if c == 0:
                            for s in range(SL):
                                ready(("ov", tag, b * SL + s))
                        for s in range(SL):
                            mm = pe.transpose(t.ap[:, s * 128:(s + 1) * 128], oT[:, b, s, c * 128:(c + 1) * 128], ident)
                        mm.then_inc(t.filled, 1)
                        if c % 2:
                            yield
                    t = claim(pe, ("onT", tag, b), ring[0])
                    for c in range(NC):
                        ready(("on", tag, b, c))
                        mm = pe.transpose(t.ap[:, c * 128:(c + 1) * 128], on[:, b, c], ident)
                    mm.then_inc(t.filled, 1)
                    yield
                    ready(("onT", tag, b))
                    token_major(("y", l, b), onT[:, b], par_of("b_wp") if tag == "b" else par_of("e_wo"))
                    yield
                if l == 2:
                    yield
                if l == 3:
                    for c in range(NC):
                        t = claim(pe, ("nq", b, c), ring[0])
                        if c == 0:
                            for s in range(SL):
                                ready(("nt", s, b))
                        for s in range(SL):
                            mm = pe.transpose(t.ap[:, s * 128:(s + 1) * 128], oT[:, b, s, c * 128:(c + 1) * 128], ident)
                        mm.then_inc(t.filled, 1)
                        if c % 2:
                            yield
                    for _ in range(5):
                        yield

            weave(context, begin, bulk, end)

        @block.vector
        def _(dve):
            steps = [0]

            def link(ins):
                steps[0] += 1
                ins.then_inc(dve_step, 1)
                dve.wait_ge(dve_step, steps[0])

            def full(key):
                t = tiles[key]
                dve.wait_ge(t.filled, t.nth)
                return t

            def ready(key):
                t = tiles[key]
                dve.wait_ge(t.drained, t.nth)

            v = nc.vector
            flat = lambda a: a.rearrange("p c d -> p (c d)")

            def statistics(l, b):
                residual_there(dve, l, b)
                for c in range(NC):
                    ins = v.bn_stats(bn[:, b, c], X[:, b, c])
                link(ins)
                for c in range(NC):
                    ins = v.bn_aggr(mv[:, b, c], bn[:, b, c])
                ins.then_inc(stats_ready, 1)

            def normalise(l, b):
                dve.wait_ge(rstd_ready, l * B + b + 1)
                dve.wait_ge(stats_ready, l * B + b + 1)
                for c in range(NC):
                    ins = v.tensor_scalar(xn[:, b, c], X[:, b, c], mv[:, b, c, 0:1], rstd[:, b, c:c + 1],
                                          ALU.subtract, ALU.mult)
                ins.then_inc(xn_ready, 1)

            def residual(l, b, biased):
                t = full(("y", l, b))
                if biased:
                    dve.wait_ge(bias_ready, biased * B - B + b + 1)
                v.tensor_tensor(flat(X[:, b]), t.ap, flat((R if biased else X)[:, b]), ALU.add).then_inc(t.drained, 1)

            def low_part(b, which, at, key, src, bias, n_hi):
                dve.wait_ge(hi_ready, n_hi)
                ins = v.scalar_tensor_tensor(out=lo[:, b, which, at], in0=src, scalar=bias, in1=hi[:, b, which, at],
                                             op0=ALU.add, op1=ALU.subtract)
                if key:
                    ins.then_inc(tiles[key].drained, 1)
                else:
                    ins.then_inc(lo_ready, 1)

            def context_rows(tag, b):
                t = full(("kc", tag, b))
                for g in range(G):
                    r = slice(32 * g, 32 * g + 32)
                    ins = v.tensor_tensor(kbd[r, b, :, g * KC:(g + 1) * KC],
                                          t.ap[r, 0:SL * KC].rearrange("p (s k) -> p s k", s=SL),
                                          kadd[r, b].unsqueeze(1).to_broadcast([32, SL, KC]), ALU.add)
                ins.then_inc(t.drained, 1)

            def maximum(tag, j, c, g):
                b, s = j // SL, j % SL
                t = full(("mx", tag, j, c, g))
                if g < 0:
                    src = t.ap[:, 0:G * KC].rearrange("p (g k) -> p g k", g=G)
                    dst = (Mx[:, b, s, c].rearrange("p (g j) -> p g j", g=G)[:, :, 0] if tag == "b"
                           else Mp[:, j % 2, c * G:(c + 1) * G])
                else:
                    src = t.ap
                    dst = Mn[:, j % 2, c * G + g:c * G + g + 1]
                v.tensor_reduce(dst, src, AX.X, ALU.max).then_inc(t.drained, 1)
                if (c, g) == max_list(tag, j)[-1] and tag == "e":
                    for g in groups_of(tag):
                        ready(("mx", tag, j, NC - 1, g))
                    v.tensor_tensor(Mx[:, b, s].rearrange("p c (g j) -> p c g j", g=G)[:, :, :, 0],
                                    Mp[:, j % 2].rearrange("p (c g) -> p c g", c=NC),
                                    Mn[:, j % 2].rearrange("p (c g) -> p c g", c=NC), ALU.max).then_inc(mx_ready, 1)

            def shift(tag, j):
                b, s = j // SL, j % SL
                t = full(("mT", tag, j))
                v.tensor_tensor(qst[:, b, s], t.ap.bitcast(F16)[:, 0:S], qst[:, b, s], ALU.add).then_inc(t.drained, 1)

            def heads(tag, l, b):
                def start():
                    for j in range(LEADING[tag] if tag == "b" else 0):
                        for m in max_list(tag, j):
                            maximum(tag, j, *m)
                    ready(("stq", tag, 0, 0))
                    shift(tag, 0)

                def half(j, n, keys):
                    for m in ahead(tag, j, n):
                        maximum(tag, *m)
                    if n == shift_step(tag) and j + 1 < B * SL:
                        ready(("stq", tag, (j + 1) // SL, (j + 1) % SL))
                        shift(tag, j + 1)

                yield from head_bulk(tag, l, b, start, half)

            def context():
                for _ in range(3):
                    yield
                dve.wait_ge(par_in[1], 16)
                dve.wait_ge(small_in, 32)
                dve.wait_ge(presets, 1)
                for b in range(B):
                    v.tensor_scalar(kadd[:, b], mask_u[:, b], par_of("kmask"), par_of("kconst"), ALU.mult,
                                    ALU.add).then_inc(kadd_ready, 1)
                    low_part(b, 1, slice(S, PK), ("kT", 1, b), tiles[("kT", 1, b)].ap[:, 0:KC], par_of("b_kb"), b + 1)
                    t = full(("v", 1, b))
                    v.tensor_tensor(vhead[0:KC, b, NC, :, 0:HD], t.ap[0:KC, 0:128].rearrange("p (h d) -> p h d", h=H),
                                    par_of("b_vb")[0:KC].rearrange("p (h d) -> p h d", h=H), ALU.add).then_inc(t.drained, 1)
                yield
                for b in range(B):
                    dve.wait_ge(kadd_ready, b + 1)
                    context_rows("b", b)
                yield

            lg, top, gt, eq, run, sel, ex, w, df, sc = small
            n_gt, wsum, winv = thin
            def begin(l, b):
                if (l, b) == (5, 0):
                    for _ in range(LAST_IDLE):
                        yield
                if (l, b) == CONTEXT_AT:
                    dve.wait_ge(ctx_in, 16)
                    link(v.tensor_copy(lens_f[:, :], lens_i[:, :]))
                    link(v.tensor_tensor(maxlen[:, :], lens_f[:, 0:1], lens_f[:, 1:2], ALU.max))
                    for i in range(B):
                        v.tensor_scalar(posm[:, i], par_of("posrow"), lens_f[:, i:i + 1], None, ALU.is_lt)
                        v.tensor_scalar(kpast[:, i], par_of("posrow"), maxlen[:, 0:1], par_of("kmask"), ALU.is_ge, ALU.mult)
                        link(v.tensor_scalar(vkeep[:, i:i + 1], par_of("pos"), lens_f[:, i:i + 1], None, ALU.is_lt))
                        v.tensor_scalar(kadd[:, i], kpast[:, i], par_of("kconst"), None, ALU.add).then_inc(kadd_ready, 1)
                        v.tensor_scalar(vhead[0:KC, i, NC, :, 0:HD], ctxk[:, i].rearrange("p (h d) -> p h d", h=H),
                                        vkeep[0:KC, i:i + 1], None, ALU.mult).then_inc(vpast_ready, 1)
                        dve.wait_ge(kadd_ready, B + 2 * i + 1)
                        v.tensor_tensor(kpast[:, i], par_of("ctxT")[:, i * KC:(i + 1) * KC], posm[:, i],
                                        ALU.mult).then_inc(kadd_ready, 1)
                statistics(l, b)
                yield
                yield
                if (l, b) == CONTEXT_AT:
                    for i in range(B):
                        dve.wait_ge(kadd_ready, B + 2 * i + 2)
                        low_part(i, 1, slice(S, PK), None, kpast[:, i], 0.0, 2 * B + i + 1)
                if l == 5 and b == 0:
                    dve.wait_ge(par_in[6], 16)
                    link(v.tensor_scalar(n0[:, :], par_of("f_th"), 1.0 / TWO_PI, ROUND, ALU.mult, ALU.add))
                    link(v.tensor_scalar(n0[:, :], n0[:, :], -ROUND, None, ALU.add))
                    link(v.scalar_tensor_tensor(out=fold[:, :], in0=n0[:, :], scalar=-PI_A, in1=par_of("f_th"), op0=ALU.mult, op1=ALU.add))
                    link(v.scalar_tensor_tensor(out=fold[:, :], in0=n0[:, :], scalar=-PI_B, in1=fold[:, :], op0=ALU.mult, op1=ALU.add))
                    link(v.scalar_tensor_tensor(out=fold[:, :], in0=n0[:, :], scalar=-PI_C, in1=fold[:, :], op0=ALU.mult, op1=ALU.add))
                    link(v.tensor_scalar(fold[:, :], fold[:, :], float(TURN / 2), -float(TURN / 2), ALU.min, ALU.max))
                    link(v.scalar_tensor_tensor(out=absr[:, :], in0=fold[:, :], scalar=-1.0, in1=fold[:, :], op0=ALU.mult, op1=ALU.max))
                    link(v.tensor_scalar(phs[:, :], fold[:, :], 1.0 / TWO_PI, None, ALU.mult))
                    v.scalar_tensor_tensor(out=phs[:, :], in0=par_of("f_b1"), scalar=0.1 / TWO_PI, in1=phs[:, :], op0=ALU.mult,
                                           op1=ALU.add).then_inc(phase_ready, 1)
                    v.tensor_scalar(cosn[:, :], absr[:, :], -1.0, np.pi / 2, ALU.mult, ALU.add).then_inc(fold_ready, 1)
                normalise(l, b)
                yield
                if (l, b) == CONTEXT_AT:
                    for i in range(B):
                        context_rows("e", i)
                yield
                yield
                if l == 0:
                    t = full(("kT", 0, b))
                    v.tensor_copy(kT[:, b], t.ap).then_inc(t.drained, 1)
                    yield
                if l == 1:
                    low_part(b, 0, slice(0, S), ("qT", l, b), tiles[("qT", l, b)].ap, par_of("b_qb"), B + b + 1)
                    yield
                    yield
                    yield
                if l == 2:
                    t = full(("lg", b))
                    v.tensor_copy(lg[:, b], t.ap[:, 0:NC * NE].rearrange("p (c e) -> p c e", c=NC)).then_inc(t.drained, 1)
                    ready(("lg", b))
                    for c in range(NC):
                        ins = v.max(top[:, b, c], lg[:, b, c])
                    link(ins)
                    best = top[:, b, :, 0:1].to_broadcast([128, NC, NE])
                    second = top[:, b, :, 1:2].to_broadcast([128, NC, NE])
                    v.tensor_tensor(df[:, b], lg[:, b], best, ALU.subtract).then_inc(diff_ready, 1)
                    v.tensor_tensor(gt[:, b], lg[:, b], second, ALU.is_gt)
                    link(v.tensor_tensor(eq[:, b], lg[:, b], second, ALU.is_equal))
                    v.tensor_reduce(n_gt[:, b], gt[:, b], AX.X, ALU.add)
                    link(v.tensor_tensor_scan(run[:, b].rearrange("p c e -> p (c e)"), par_of("c_reset"),
                                              eq[:, b].rearrange("p c e -> p (c e)"), 0.0, ALU.mult, ALU.add))
                    yield
                    link(v.tensor_tensor(run[:, b], run[:, b], n_gt[:, b].unsqueeze(2).to_broadcast([128, NC, NE]), ALU.add))
                    link(v.scalar_tensor_tensor(out=sel[:, b], in0=run[:, b], scalar=2.0, in1=eq[:, b], op0=ALU.is_le,
                                                op1=ALU.mult))
                    link(v.tensor_tensor(sel[:, b], sel[:, b], gt[:, b], ALU.add))
                    dve.wait_ge(e_ready, b + 1)
                    link(v.tensor_tensor(w[:, b], ex[:, b], sel[:, b], ALU.mult))
                    link(v.tensor_reduce(wsum[:, b], w[:, b], AX.X, ALU.add))
                    link(v.reciprocal(winv[:, b], wsum[:, b]))
                    v.tensor_tensor(sc[:, b], w[:, b], winv[:, b].unsqueeze(2).to_broadcast([128, NC, NE]),
                                    ALU.mult).then_inc(score_ready, 1)
                    yield
                    t = full(("sT", b))
                    dve.wait_ge(hi16_ready, b + 1)
                    v.tensor_tensor(s16[32:32 + NE, b], t.ap[0:NE], s16[0:NE, b], ALU.subtract).then_inc(t.drained, 1)
                    yield
                if l == 3:
                    if b == 0:
                        dve.wait_ge(par_in[4], 16)
                        dve.wait_ge(par_in[5], 16)
                    for which, (cn, sn) in enumerate((("d_cosq", "d_sinq"), ("d_cosk", "d_sink"))):
                        t = full(("r", b, 2 * which))
                        if which:
                            dve.wait_ge(rot_ready, 2 * b + 1)
                        v.tensor_tensor(rot[:, b, 2], t.ap, par_of(cn), ALU.mult).then_inc(t.drained, 1)
                        u = full(("r", b, 2 * which + 1))
                        v.tensor_tensor(rot[:, b, 3], u.ap, par_of(sn), ALU.mult).then_inc(u.drained, 1)
                        dve.wait_ge(t.drained, t.nth)
                        dve.wait_ge(u.drained, u.nth)
                        v.tensor_tensor(rot[:, b, which], rot[:, b, 2], rot[:, b, 3], ALU.add).then_inc(rot_ready, 1)
                        yield
                    t = full(("gate", b))
                    dve.wait_ge(th_ready, b + 1)
                    v.scalar_tensor_tensor(out=flat(th[b]), in0=flat(th[b]), scalar=1.0, in1=t.ap, op0=ALU.add,
                                           op1=ALU.mult).then_inc(t.drained, 1)
                    for which in range(2):
                        dve.wait_ge(hi_ready, 3 * B + 2 * b + which + 1)
                        dve.wait_ge(rot_ready, 2 * b + which + 1)
                        v.tensor_tensor(lo[:, b, which, 0:S], rot[:, b, which], hi[:, b, which, 0:S],
                                        ALU.subtract).then_inc(lo_ready, 1)
                    yield
                    yield
                    yield
                    yield
                    yield
                    for c in range(NC - 1):
                        t = full(("kv", b, c))
                        if c == 0:
                            v.tensor_tensor(state[b][:, 0], t.ap[:, 0:128], par_of("d_gm"), ALU.mult).then_inc(t.drained, 1)
                        else:
                            if c == 1:
                                ready(("kv", b, 0))
                            else:
                                dve.wait_ge(state_ready, b * (NC - 2) + c - 1)
                            v.tensor_tensor(stmp[b], t.ap[:, 0:128], state[b][:, c - 1], ALU.add).then_inc(t.drained, 1)
                            dve.wait_ge(t.drained, t.nth)
                            v.tensor_tensor(state[b][:, c], stmp[b], par_of("d_gm"), ALU.mult).then_inc(state_ready, 1)
                    yield
                    yield
                    yield
                if l == 4:
                    for which, name in ((1, "kT"), (0, "qT")):
                        low_part(b, which, slice(0, S), (name, l, b), tiles[(name, l, b)].ap, 0.0,
                                 5 * B + 2 * b + (2 - which))
                    for _ in range(6):
                        yield
                    if b == 0:
                        for n, m in enumerate(max_list("e", 0)):
                            maximum("e", 0, *m)
                            if n % 2:
                                yield
                if l == 5:
                    def wrap(j):
                        off = wrapped(b, j)
                        if b == 0:
                            t = full(("f1", b, j))
                            v.tensor_scalar(PT[:, NJ * b + j], t.ap, par_of("f_b1")[:, j:j + 1], None, ALU.add)
                            if j == 0:
                                dve.wait_ge(phase_ready, 1)
                            v.tensor_scalar(off, t.ap, 0.1 / TWO_PI, phs[:, j:j + 1], ALU.mult, ALU.add).then_inc(t.drained, 1)
                        ready(("f1", b, j))
                        if j:
                            dve.wait_ge(wrap_ready, b * NJ + j)
                        link(v.tensor_scalar(kT[:, b], off, ROUND, None, ALU.add))
                        v.scalar_tensor_tensor(out=off, in0=kT[:, b], scalar=-ROUND, in1=off, op0=ALU.add,
                                               op1=ALU.subtract).then_inc(wrap_ready, 1)

                    def mix(j):
                        dve.wait_ge(sine_ready, b * NJ + j + 1)
                        v.scalar_tensor_tensor(out=PT[:, NJ * b + j], in0=wrapped(b, j), scalar=amp[:, j:j + 1],
                                               in1=PT[:, NJ * b + j], op0=ALU.mult, op1=ALU.add).then_inc(mix_ready, 1)

                    for j in range(NJ):
                        wrap(j)
                        if b == 1 and j:
                            mix(j - 1)
                        yield
                    if b == 0:
                        for _ in range(FF_PAUSE + 1):
                            yield
                        dve.wait_ge(sinv_ready, 1)
                        v.tensor_tensor(a1[:, :], cos_v[:, :], par_of("f_wr"), ALU.mult)
                        link(v.tensor_tensor(a2[:, :], sin_v[:, :], par_of("f_wi"), ALU.mult))
                        link(v.tensor_tensor(a1[:, :], a1[:, :], a2[:, :], ALU.add))
                        link(v.scalar_tensor_tensor(out=amp[:, :], in0=a1[:, :], scalar=0.1, in1=par_of("f_wi"),
                                                    op0=ALU.mult, op1=ALU.mult))
                        for n in range(1, 12):
                            if n in MIX_AT:
                                mix(MIX_AT.index(n))
                            yield
                    else:
                        mix(NJ - 1)
                        yield
                    yield
                    yield
                    residual(5, b, 4)
                    yield

            def self_attention(b):
                for c in range(NC):
                    t = full(("s", b, c))
                    v.tensor_reduce(negmax[:, b, c:c + 1], t.ap, AX.X, ALU.max, negate=True).then_inc(max_ready, 1)
                    yield
                for c in range(NC):
                    if c % 2 == 0:
                        t = full(("pT", b, c))
                        v.tensor_copy(PT[:, b * NC + c], t.ap).then_inc(t.drained, 1)
                    yield
                ready(("s", b, NC - 1))
                v.reciprocal(rinv[:, b], rowsum[:, b]).then_inc(rinv_ready, 1)
                t = full(("o", 0, b))
                dve.wait_ge(rinv_ready, b + 1)
                v.tensor_tensor(flat(Osb[:, b]).rearrange("p (d j) -> p j d", j=NC),
                                t.ap.rearrange("p (c d) -> p c d", c=NC),
                                rinv[:, b].unsqueeze(2).to_broadcast([128, NC, 128]), ALU.mult).then_inc(t.drained, 1)
                yield

            scaled = [0]

            def experts(b):
                if b == 0:
                    dve.wait_ge(*quads_used[B * SL - 1])
                for e in range(NE):
                    t = full(("sb", e, b))
                    for hf in range(2):
                        n = scaled[0]
                        ready(("h", e, b, hf))
                        if n >= 8:
                            dve.wait_ge(g_used, n - 7)
                        ins = v.tensor_tensor(big[:, 8 + n % 8], t.ap, big[:, n % 8], ALU.mult)
                        ins.then_inc(g_ready if hf == 0 else t.drained, 1)
                        scaled[0] += 1
                    yield
                    yield

            def retention(b):
                if b == 0:
                    full(("y", 2, B - 1))
                for n in range(H * b, H * b + H):
                    j, g = n // G, n % G
                    t = full(("dg", j, g))
                    if n >= 8:
                        used_diagonals(dve, n // 4 - 2)
                    v.tensor_tensor(big[:, n % 8].rearrange("p (c q) -> p c q", c=NC), t.ap.rearrange("p (c q) -> p c q", c=NC),
                                    par_of("d_tri").unsqueeze(1).to_broadcast([128, NC, 128]), ALU.mult).then_inc(t.drained, 1)
                    if n % 2:
                        t = full(("of", j, g))
                        if n >= 4:
                            dve.wait_ge(off_used, n - 3)
                        v.tensor_scalar(Aoff[n % 4].bitcast(I32), t.wide.rearrange("p a q -> p (a q)")[:, 0:768].bitcast(I32),
                                        0x7FFFFFFF, None, ALU.bitwise_and).then_inc(t.drained, 1)
                    yield

            def bulk(l, b):
                yield from (self_attention(b) if l == 0 else heads("b", l, b) if l == 1 else experts(b) if l == 2
                            else retention(b) if l == 3 else heads("e", l, b))

            dens, fac, ss, rr, tmp, fin = f16h
            num, sq = xn, on
            by_slot = lambda a: a.rearrange("p (g s d) -> p s g d", g=G, s=SL)

            def end(l, b):
                for _ in range(idle(l, b)):
                    yield
                if l == 0:
                    residual(0, b, 1)
                    yield
                if l in (1, 4):
                    tag = "b" if l == 1 else "e"
                    for c in range(NC):
                        t = full(("on", tag, b, c))
                        ps = t.ap.rearrange("p (s g j) -> p s g j", s=SL, g=G)
                        link(v.reciprocal(rden[:, b, c], ps[:, :, :, HD]))
                        v.tensor_tensor(by_slot(on[:, b, c]), ps[:, :, :, 0:HD],
                                        rden[:, b, c].unsqueeze(3).to_broadcast([128, SL, G, HD]),
                                        ALU.mult).then_inc(t.drained, 1)
                        if c % 2:
                            yield
                    yield
                    residual(l, b, {"b": 2, "e": 3}[tag])
                    yield
                if l == 2:
                    residual(2, b, 0)
                    yield
                if l == 3:
                    ready(("cr", b))
                    for c in range(NC):
                        t = full(("nq", b, c))
                        ps = t.ap.rearrange("p (s g j) -> p s g j", s=SL, g=G)
                        v.tensor_copy(dens[:, b, c * H:(c + 1) * H].rearrange("p (g s) -> p s g", g=G), ps[:, :, :, HD])
                        if c == 0:
                            v.tensor_copy(by_slot(num[:, b, c]), ps[:, :, :, 0:HD]).then_inc(t.drained, 1)
                        else:
                            v.tensor_tensor(by_slot(num[:, b, c]), ps[:, :, :, 0:HD], by_slot(cross[:, b, c]),
                                            ALU.add).then_inc(t.drained, 1)
                        if c % 2:
                            yield
                    for c in range(NC):
                        ready(("nq", b, c))
                    v.tensor_tensor(flat(sq[:, b]), flat(num[:, b]), flat(num[:, b]), ALU.mult).then_inc(num_ready, 1)
                    link(v.tensor_tensor(dens[:, b], dens[:, b], par_of("d_td"), ALU.mult))
                    link(v.tensor_scalar(dens[:, b], dens[:, b], 1.0, 50000.0, ALU.max, ALU.min))
                    link(v.reciprocal(rr[:, b], dens[:, b]))
                    link(v.tensor_tensor(fac[:, b], rr[:, b], par_of("d_tn"), ALU.mult))
                    yield
                    dve.wait_ge(num_ready, b + 1)
                    v.tensor_reduce(ss[:, b], flat(sq[:, b]).rearrange("p (n d) -> p n d", d=HD), AX.X, ALU.add)
                    link(v.tensor_tensor(tmp[:, b], fac[:, b], fac[:, b], ALU.mult))
                    link(v.tensor_tensor(ss[:, b], ss[:, b], tmp[:, b], ALU.mult))
                    v.tensor_scalar(ss[:, b], ss[:, b], 1.0 / HD, RMS_EPS, ALU.mult, ALU.add).then_inc(rms_ready, 1)
                    yield
                    yield
                    dve.wait_ge(root_ready, b + 1)
                    link(v.reciprocal(fin[:, b], fin[:, b]))
                    link(v.scalar_tensor_tensor(out=fin[:, b], in0=fin[:, b], scalar=0.5, in1=fac[:, b], op0=ALU.mult,
                                                op1=ALU.mult))
                    dve.wait_ge(gated_ready, b + 1)
                    perhead = flat(th[b]).rearrange("p (n d) -> p n d", d=HD)
                    link(v.tensor_tensor(perhead, perhead, fin[:, b].unsqueeze(2).to_broadcast([128, NC * H, HD]), ALU.mult))
                    yield
                    v.tensor_tensor(flat(X[:, b]), flat(X[:, b]), flat(th[b]), ALU.add).then_inc(res_ready, 1)
                    yield

            weave(context, begin, bulk, end)

        @block.scalar
        def _(act):
            a = nc.scalar

            def full(key):
                t = tiles[key]
                act.wait_ge(t.filled, t.nth)
                return t

            def ready(key):
                t = tiles[key]
                act.wait_ge(t.drained, t.nth)

            def evac(key, dst, n=S, scale=1.0, bias=0.0):
                t = full(key)
                a.activation(dst, t.ap[:, 0:n], ACT.Identity, bias=bias, scale=scale).then_inc(t.drained, 1)

            def high(key, dst, src, bias):
                if key:
                    full(key)
                a.activation(dst, src, ACT.Identity, bias=bias).then_inc(hi_ready, 1)

            nb = [0]

            def heads(tag, l, b):
                def start():
                    if tag == "e":
                        full(("nt", SL - 1, B - 1))

                def half(j, n, keys):
                    k, nk, past = keys[n // 2]
                    t = full(("sc", tag, j, k, n % 2))
                    if nb[0] >= 8:
                        act.wait_ge(*quads_used[nb[0] // 2 - 4])
                    buf = nb[0] % 8
                    a.activation(big[0:nk, 2 * buf:2 * buf + 2], t.wide[0:nk], ACT.Exp, scale=SCALE).then_inc(t.drained, 1)
                    nb[0] += 1
                    done = j - 2 if tag == "b" else j - 1
                    if n == (0 if tag == "b" else 2) and done >= 0:
                        evac(("ov", tag, done), oT[:, done // SL, done % SL])

                yield from head_bulk(tag, l, b, start, half)
                if b == B - 1:
                    for j in range(B * SL - (2 if tag == "b" else 1), B * SL):
                        evac(("ov", tag, j), oT[:, j // SL, j % SL])

            def context():
                for _ in range(3):
                    yield
                act.wait_ge(par_in[1], 16)
                act.wait_ge(presets, 1)
                for b in range(B):
                    high(("kT", 1, b), hi[:, b, 1, S:PK], tiles[("kT", 1, b)].ap[:, 0:KC], par_of("b_kb"))
                yield
                yield

            def begin(l, b):
                if (l, b) == (5, 0):
                    for _ in range(LAST_IDLE):
                        yield
                yield
                if (l, b) == CONTEXT_AT:
                    for i in range(B):
                        act.wait_ge(kadd_ready, B + 2 * i + 2)
                        high(None, hi[:, i, 1, S:PK], kpast[:, i], 0.0)
                yield
                yield
                yield
                evac(("xT", l, b), xnT[:, b])
                yield
                if l == 0:
                    evac(("qT", 0, b), qT[:, b], scale=SCALE)
                    evac(("v", 0, b), vtok[:, b].rearrange("p c d -> p (c d)"))
                    yield
                if l == 1:
                    high(("qT", l, b), hi[:, b, 0, 0:S], tiles[("qT", l, b)].ap, par_of("b_qb"))
                    yield
                    for s in range(SL):
                        evac(("stq", "b", b, s), qst[:, b, s], bias=par_of("qconst"))
                        if s % 2:
                            yield
                if l == 2:
                    yield
                    act.wait_ge(diff_ready, b + 1)
                    a.activation(small[6][:, b], small[8][:, b], ACT.Exp).then_inc(e_ready, 1)
                    yield
                    t = full(("sT", b))
                    a.activation(s32[:, b], t.ap[0:NE], ACT.Identity)
                    a.activation(s16[0:NE, b], t.ap[0:NE], ACT.Identity).then_inc(hi16_ready, 1)
                    yield
                if l == 3:
                    yield
                    yield
                    evac(("v", 3, b), vtok[:, b].rearrange("p c d -> p (c d)"))
                    t = full(("gate", b))
                    a.activation(th[b].rearrange("p c d -> p (c d)"), t.ap, ACT.Tanh, scale=0.5).then_inc(th_ready, 1)
                    for which in range(2):
                        act.wait_ge(rot_ready, 2 * b + which + 1)
                        a.activation(hi[:, b, which, 0:S], rot[:, b, which], ACT.Identity).then_inc(hi_ready, 1)
                    yield
                    evac(("ktok", b), ktok[:, b].rearrange("p c d -> p (c d)"))
                    for s in range(SL):
                        evac(("stk", "d", b, s), kst[:, b, s])
                        if s % 2:
                            yield
                    for s in range(SL):
                        evac(("stq", "d", b, s), qst[:, b, s])
                        if s % 2:
                            yield
                    yield
                    yield
                    t = full(("cr", b))
                    a.activation(cross[:, b, 1:NC].rearrange("p c d -> p (c d)"), t.ap[:, 128:512],
                                 ACT.Identity).then_inc(t.drained, 1)
                    yield
                if l == 4:
                    high(("kT", l, b), hi[:, b, 1, 0:S], tiles[("kT", l, b)].ap, 0.0)
                    high(("qT", l, b), hi[:, b, 0, 0:S], tiles[("qT", l, b)].ap, 0.0)
                    yield
                    for s in range(SL):
                        evac(("stk", "e", b, s), kst[:, b, s], bias=par_of("kconst"))
                        if s % 2:
                            yield
                    for s in range(SL):
                        evac(("stq", "e", b, s), qst[:, b, s], bias=par_of("qconst"))
                        if s % 2:
                            yield
                    t = full(("v", l, b))
                    a.activation(vhead[:, b, 0:NC, :, 0:HD],
                                 t.ap.rearrange("p (c h d) -> p c h d", c=NC, d=HD), ACT.Identity).then_inc(t.drained, 1)
                    yield
                    if b == 0:
                        for _ in range(len(max_list("e", 0)) // 2):
                            yield
                if l == 5:
                    def sine(j):
                        act.wait_ge(wrap_ready, b * NJ + j + 1)
                        o = wrapped(b, j)
                        a.activation(o, o, ACT.Sin, scale=-TURN).then_inc(sine_ready, 1)

                    def relu(j):
                        act.wait_ge(mix_ready, b * NJ + j + 1)
                        a.activation(PT[:, NJ * b + j], PT[:, NJ * b + j], ACT.Relu).then_inc(act_ready, 1)

                    for j in range(NJ):
                        if b == 1:
                            t = full(("f1", b, j))
                            a.activation(PT[:, NJ * b + j], t.ap, ACT.Identity, bias=par_of("f_b1")[:, j:j + 1])
                            a.activation(wrapped(b, j), t.ap, ACT.Identity, bias=phs[:, j:j + 1],
                                         scale=0.1 / TWO_PI).then_inc(t.drained, 1)
                            if j >= 1:
                                sine(j - 1)
                            if j >= 2:
                                relu(j - 2)
                        yield
                    if b == 0:
                        for _ in range(FF_PAUSE):
                            yield
                        act.wait_ge(fold_ready, 1)
                        a.activation(sin_v[:, :], fold[:, :], ACT.Sin)
                        a.activation(cos_v[:, :], cosn[:, :], ACT.Sin).then_inc(sinv_ready, 1)
                        for j in range(NJ):
                            sine(j)
                        for n in range(12):
                            if n - 1 in MIX_AT:
                                relu(MIX_AT.index(n - 1))
                            yield
                    else:
                        sine(NJ - 1)
                        relu(NJ - 2)
                        relu(NJ - 1)
                        yield
                    yield
                    yield
                    yield

            def self_attention(b):
                for c in range(NC):
                    t = full(("s", b, c))
                    act.wait_ge(max_ready, b * NC + c + 1)
                    a.activation(big[:, b * NC + c], t.ap, ACT.Exp, bias=negmax[:, b, c:c + 1],
                                 accum_out=rowsum[:, b, c:c + 1]).then_inc(t.drained, 1)
                    yield
                for c in range(NC):
                    if c % 2:
                        evac(("pT", b, c), PT[:, b * NC + c])
                    yield
                yield

            hidden = [0]

            def experts(b):
                if b == 0:
                    act.wait_ge(*quads_used[B * SL - 1])
                for e in range(NE):
                    for hf in range(2):
                        n = hidden[0]
                        t = full(("h", e, b, hf))
                        if n >= 8 and hf == 0:
                            before = (n - 8) // 2
                            ready(("sb", before % NE, before // NE))
                        a.activation(big[:, n % 8], t.ap, ACT.Relu,
                                     bias=par_of("c_b1")[:, 2 * e + hf:2 * e + hf + 1]).then_inc(t.drained, 1)
                        hidden[0] += 1
                    yield
                    yield

            def retention(b):
                if b == 0:
                    full(("y", 2, B - 1))
                for n in range(H * b, H * b + H):
                    j, g = n // G, n % G
                    ready(("dg", j, g))
                    if n >= 8:
                        used_diagonals(act, n // 4 - 2)
                    a.activation(big[:, 8 + n % 8], big[:, n % 8], ACT.Abs).then_inc(absd_ready, 1)
                    if n % 2 == 0:
                        t = full(("of", j, g))
                        if n >= 4:
                            act.wait_ge(off_used, n - 3)
                        a.activation(Aoff[n % 4], t.wide.rearrange("p a q -> p (a q)")[:, 0:768], ACT.Abs).then_inc(t.drained, 1)
                    if n % 4 == 3 and n >= 7:
                        i = n // 4 - 1
                        evac(("nt", i % SL, i // SL), oT[:, i // SL, i % SL])
                    yield
                if b == B - 1:
                    evac(("nt", SL - 1, B - 1), oT[:, B - 1, SL - 1])

            def bulk(l, b):
                yield from (self_attention(b) if l == 0 else heads("b", l, b) if l == 1 else experts(b) if l == 2
                            else retention(b) if l == 3 else heads("e", l, b))

            def end(l, b):
                for n in range(idle(l, b) + (1, 4, 1, 7, 4)[l]):
                    if l in (1, 4) and n == idle(l, b) + 2:
                        evac(("onT", "b" if l == 1 else "e", b), onT[:, b])
                    if l == 3 and n == idle(l, b) + 4:
                        act.wait_ge(rms_ready, b + 1)
                        a.activation(f16h[5][:, b], f16h[2][:, b], ACT.Sqrt).then_inc(root_ready, 1)
                    yield

            weave(context, begin, bulk, end)

        @block.gpsimd
        def _(pool):
            p = nc.gpsimd
            steps = [0]

            def link(ins):
                steps[0] += 1
                ins.then_inc(pool_step, 1)
                pool.wait_ge(pool_step, steps[0])

            def norm(l, b):
                pool.wait_ge(stats_ready, l * B + b + 1)
                link(p.tensor_scalar(veps[:, b], mv[:, b, :, 1], LN_EPS, None, ALU.add))
                p.tensor_tensor(rstd[:, b], veps[:, b], neghalf[:, 0:NC], ALU.pow).then_inc(rstd_ready, 1)
                bias = {0: "a_bp", 1: "b_bp", 4: "e_bo", 5: "f_b2"}.get(l)
                if bias:
                    p.tensor_tensor(R[:, b], X[:, b], par_of(bias).unsqueeze(1).to_broadcast([128, NC, 128]),
                                    ALU.add).then_inc(bias_ready, 1)

            link(p.memset(neghalf[:, :], -0.5))
            link(p.memset(kbd[:, :, :, :].rearrange("p b s k -> p (b s k)"), 0.0))
            link(p.memset(vst[:, :, :, :].rearrange("p b c j -> p (b c j)"), 0.0))
            p.memset(vhead[:, :, :, :, HD].rearrange("p b c h -> p (b c) h"), 1.0).then_inc(presets, 1)
            pool.wait_ge(par_in[0], 16)
            for b in range(B):
                norm(0, b)
            link(p.memset(Mx[:, :, :, :, :].rearrange("p b s c j -> p (b s c j)"), 0.0))
            link(p.memset(s16, 0.0))
            p.memset(kw[:, :, :, :].rearrange("p r g k -> p (r g k)").bitcast(F32), 0.0).then_inc(presets, 1)
            pool.wait_ge(par_in[1], 16)
            for b in range(B):
                norm(1, b)
            for b in range(B):
                norm(2, b)
            for b in range(B):
                norm(3, b)
                link(p.memset(vhead[:, b, 0:NC, :, HD], 0.0))
                t = tiles[("v", 3, b)]
                pool.wait_ge(t.drained, t.nth)
                p.tensor_copy(vhead[:, b, 0:NC, :, 0:HD],
                              vtok[:, b].rearrange("p c (h d) -> p c h d", h=H)).then_inc(vpad_ready, 1)
            for b in range(B):
                pool.wait_ge(num_ready, b + 1)
                t = tiles[("gate", b)]
                pool.wait_ge(t.drained, t.nth)
                flat = lambda a: a.rearrange("p c d -> p (c d)")
                p.tensor_tensor(flat(th[b]), flat(th[b]), flat(xn[:, b]), ALU.mult).then_inc(gated_ready, 1)
                pool.wait_ge(res_ready, b + 1)
                p.memset(vhead[:, b, 0:NC, :, HD], 1.0).then_inc(ones_ready, 1)
                if b == 0:
                    pool.wait_ge(par_in[6], 16)
                norm(4, b)
            for b in range(B):
                norm(5, b)

        @block.sync
        def _(sp):
            def load_chunk(n):
                a0 = P32[CHUNKS[n][0][0]][0]
                a1 = P32[CHUNKS[n][-1][0]][1]
                at = sum(w for ch in CHUNKS[:n] for _, w in ch)
                sp.dma_start(params[:, a0:a1], par[:, at:at + a1 - a0]).then_inc(par_in[n], 16)

            for b in range(B):
                sp.dma_start(X[:, b], x[b].rearrange("(c p) d -> p c d", p=128)).then_inc(x_in[b], 16)
                if b == 0:
                    load_chunk(0)
            sp.dma_start(halves[:, :], half).then_inc(half_in, 16)
            load_chunk(1)
            sp.dma_start(ctxk[:, :, :], ctx_kd.rearrange("b k d -> k b d")).then_inc(ctx_in, 16)
            sp.dma_start(lens_i[:, :], lens.unsqueeze(0).to_broadcast([128, B])).then_inc(small_in, 16)
            sp.dma_start(mask_u[:, :, :], maskb.unsqueeze(0).to_broadcast([128, B, KC])).then_inc(small_in, 16)
            for n in range(2, len(CHUNKS) - 1):
                load_chunk(n)
            last_scores = []
            for tag in ("d", "e"):
                for j in range(B * SL):
                    if tag == "d" and j == SL:
                        t = tiles[("y", 2, B - 1)]
                        sp.wait_ge(t.filled, t.nth)
                        load_chunk(len(CHUNKS) - 1)
                    b, s = j // SL, j % SL
                    t = tiles[("stk", tag, b, s)]
                    sp.wait_ge(t.drained, t.nth)
                    if len(last_scores) >= KR:
                        u = last_scores[-KR]
                        sp.wait_ge(u.filled, u.nth)
                    elif j == 0:
                        sp.wait_ge(presets, 2)
                    for g in range(G):
                        r = slice(32 * g, 32 * g + 32)
                        sp.dma_start(kw[r, j % KR, g], kst[r, b, s]).then_inc(kw_in[j % KR], 16)
                    last_scores.append(tiles[("of", j, G - 1) if tag == "d" else ("sc", tag, j, NC - 1, 1)])
            for b in range(B):
                residual_there(sp, 6, b)
                sp.dma_start(out[b].rearrange("(c p) d -> p c d", p=128), X[:, b]).then_inc(out_done, 16)
            sp.wait_ge(half_in, 16)
            sp.wait_ge(ctx_in, 16)
            sp.wait_ge(small_in, 32)
            for n in range(len(CHUNKS)):
                sp.wait_ge(par_in[n], 16)
            sp.wait_ge(out_done, 16 * B)


def constants():
    f = np.float32
    p = np.arange(128)
    c = {"ident": np.eye(128, dtype=f)}
    row = p % 32
    col = lambda a: a.astype(f).reshape(128, -1)
    c["kconst"] = col(np.where(row == 0, -1.0, 0.0))
    c["kmask"] = col(np.where(row == 1, -BIG, 0.0))
    c["qconst"] = col(np.where(row == 1, BIG, 0.0))
    c["pos"] = col(p)
    c["posrow"] = np.broadcast_to(np.arange(KC, dtype=f), (128, KC))
    c["c_reset"] = np.broadcast_to((np.arange(NC * NE) % NE != 0).astype(f), (128, NC * NE))
    angle = np.repeat((1.0 / 10000.0 ** np.linspace(0.0, 1.0, HD // 2)).astype(f), 2)
    turn = (np.arange(S, dtype=f)[None, :] * angle[:, None]).astype(np.float64)
    gamma = 1.0 - 2.0 ** (-5.0 - np.arange(H))
    t = np.arange(S)
    up = gamma[:, None] ** (t % 128)[None, :]
    sign = np.where(np.arange(HD) % 2 == 0, -1.0, 1.0)[:, None]
    cos, sin = np.cos(turn), np.sin(turn) * sign
    full = lambda a, d: (a[None, :, :] * d[:, None, :]).reshape(128, S).astype(f)
    c["d_cosq"], c["d_sinq"] = full(cos, up), full(sin, up)
    down = D ** -0.5 / up
    c["d_cosk"], c["d_sink"] = full(cos, down), full(sin, down)
    c["d_tri"] = (p[:, None] <= p[None, :]).astype(f)
    head = p // HD
    c["d_gm"] = ((head[:, None] == head[None, :]) * (gamma[head] ** 128)[:, None]).astype(f)
    norm = 1.0 / np.sqrt(np.cumsum(gamma[:, None] ** t[None, :], axis=1))
    tn = norm.reshape(H, NC, 128).transpose(2, 1, 0)
    td = tn * (gamma[None, None, :] ** (128.0 * np.arange(NC))[None, :, None])
    c["d_tn"], c["d_td"] = col(tn), col(td)
    ones = np.zeros((128, NC, VW))
    ones[:, :, HD:H * (HD + 1):HD + 1] = (gamma[None, :] ** (-128.0 * np.arange(NC))[:, None])[None]
    c["d_one"] = col(ones)
    half = {"ident16": np.eye(128)}
    for name, rows in (("q_hi", (8, 16)), ("q_lo", (24,)), ("k_hi", (8, 24)), ("k_lo", (16,))):
        m = np.zeros((128, SL, 128))
        for g in range(G):
            for s in range(SL):
                for d in range(HD):
                    for r in rows:
                        m[32 * g + 8 * s + d, s, 32 * g + r + d] = 1.0
        half[name] = m.reshape(128, -1)
    e = np.zeros((128, NE, 128))
    for i in range(NE):
        e[i, i] = 1.0
        e[32 + i, i] = 1.0
    half["sel_e"] = e.reshape(128, -1)
    return c, np.concatenate([half[n].astype(np.float16) for n, _ in HALVES], axis=1)


def kernel(x, ctx_1024, _lenS2, mask_BxS2_bk0, **w):
    import concourse.bacc as bacc
    from concourse.bass_utils import run_bass_kernel_spmd

    arr = {k: np.asarray(v) for k, v in w.items()}
    ctx = np.ascontiguousarray(ctx_1024)
    c, half = constants()
    bc = lambda a: np.broadcast_to(a[None, :], (128, a.shape[0]))
    c["ctxT"] = ctx.transpose(2, 0, 1).reshape(128, B * KC)
    wqkv = arr["L0_attn_w_qkv"]
    c["a_wq"], c["a_wk"], c["a_wv"] = (wqkv[n * 128:(n + 1) * 128].T for n in range(3))
    c["a_wp"], c["a_bp"] = arr["L0_attn_w_proj"].T, bc(arr["L0_attn_b_proj"])
    kvw, kvb = arr["L0_xattn_kv_w"], arr["L0_xattn_kv_b"]
    c["b_wq"], c["b_wk"], c["b_wv"] = arr["L0_xattn_q_w"].T, kvw[0:128].T, kvw[128:256].T
    c["b_wp"], c["b_bp"], c["b_vb"] = arr["L0_xattn_proj_w"].T, bc(arr["L0_xattn_proj_b"]), bc(kvb[128:256])
    c["b_qb"], c["b_kb"] = arr["L0_xattn_q_b"].reshape(128, 1), kvb[0:128].reshape(128, 1)
    c["c_wg"] = arr["L0_ffn_Wg"]
    c["c_b1"] = arr["L0_ffn_b1"].reshape(2 * NE, 128).T
    c["c_b2"] = np.concatenate([arr["L0_ffn_b2"], np.zeros((128 - NE, 128), np.float32)])
    c["c_w1"] = arr["L0_ffn_W1"].transpose(1, 0, 2).reshape(128, NE * FE)
    c["c_w2"] = arr["L0_ffn_W2"].reshape(2 * NE, 128, 128).transpose(1, 0, 2).reshape(128, NE * FE)
    swap = np.arange(128) ^ 1
    c["d_wq"], c["d_wk"] = arr["L1_attn_Wq"], arr["L1_attn_Wk"]
    c["d_wqs"], c["d_wks"] = c["d_wq"][:, swap], c["d_wk"][:, swap]
    c["d_wv"], c["d_wg"] = arr["L1_attn_Wv"], arr["L1_attn_Wg"]
    for n in "qkvo":
        c["e_w" + n] = arr["L1_xattn_w" + n].T
    c["e_bo"], c["f_b2"] = bc(arr["L1_xattn_bo"]), bc(arr["L1_ffn_b2"])
    for n, a in (("f_b1", "b1"), ("f_th", "quantum_phases"), ("f_wr", "quantum_weights_real"), ("f_wi", "quantum_weights_imag")):
        c[n] = arr["L1_ffn_" + a].reshape(NJ, 128).T
    c["f_w1"] = arr["L1_ffn_W1"]
    c["f_w2"] = arr["L1_ffn_W2"].reshape(NJ, 128, 128).transpose(1, 0, 2).reshape(128, NJ * 128)
    par = np.concatenate([c[n] for ch in CHUNKS for n, _ in ch], axis=1)
    assert par.shape == (128, WIDTH) and half.shape == (128, HWIDTH)

    nc = bacc.Bacc("TRN2", target_bir_lowering=False, num_devices=1)
    arrays = {"x_dram": np.ascontiguousarray(x), "ctx_dram": ctx, "len_dram": np.ascontiguousarray(_lenS2),
              "mask_dram": np.ascontiguousarray(mask_BxS2_bk0), "par_dram": np.ascontiguousarray(par),
              "half_dram": half}
    aps = [nc.dram_tensor(n, a.shape, mybir.dt.from_np(a.dtype), kind="ExternalInput").ap() for n, a in arrays.items()]
    out = nc.dram_tensor("out_dram", (B, S, D), F32, kind="ExternalOutput").ap()
    decoder(nc, *aps, out)
    r = run_bass_kernel_spmd(nc, [arrays], core_ids=[0])
    return r.results[0]["out_dram"]
```
